# Optimizing a Trainium2 kernel written in Bass

```python
import numpy as np
import jax
import jax.numpy as jnp

def _softmax(x, axis=-1):
    return jax.nn.softmax(x, axis=axis)

def _gelu(x):
    return jax.nn.gelu(x, approximate=True)

def _silu(x):
    return jax.nn.silu(x)

def _sigmoid(x):
    return jax.nn.sigmoid(x)

def _layernorm(x, axis=-1, eps=1e-05):
    m = jnp.mean(x, axis=axis, keepdims=True)
    v = jnp.var(x, axis=axis, keepdims=True)
    return (x - m) / jnp.sqrt(v + eps)

def _scatter_add(tgt, idx, src, axis=0):
    return tgt.at[idx].add(src)

def _segment_sum(src, seg, n):
    return jax.ops.segment_sum(src, seg, n)
kernel_name = 'mk_prb_d1_jaxref_r2_6c33f7'

def setup_inputs(seed: int=0):
    np.random.seed(seed)
    _w = jnp.asarray

    def _L0_attn_setup():
        import jax, jax.numpy as jnp
        import numpy as np

        def _parallel_scan_affine(log_a, b):
            T = log_a.shape[1]
            la, bv = (log_a, b)
            stride = 1
            while stride < T:
                la_prev = jnp.roll(la, stride, axis=1).at[:, :stride, :].set(0.0)
                bv_prev = jnp.roll(bv, stride, axis=1).at[:, :stride, :].set(0.0)
                bv = jnp.exp(la) * bv_prev + bv
                la = la + la_prev
                stride *= 2
            return bv
        key = jax.random.key(seed)
        kx, kwz, kwh = jax.random.split(key, 3)
        B, T, D = (4, 2048, 512)
        x = jax.random.normal(kx, (B, T, D), dtype=jnp.float32)
        Wz = jax.random.normal(kwz, (D, D), dtype=jnp.float32) * 0.02
        bz = jnp.zeros((D,), dtype=jnp.float32)
        Wh = jax.random.normal(kwh, (D, D), dtype=jnp.float32) * 0.02
        bh = jnp.zeros((D,), dtype=jnp.float32)
        return {'x': x, 'Wz': Wz, 'bz': bz, 'Wh': Wh, 'bh': bh}
    _L0_attn_in = _L0_attn_setup()

    def _L0_ffn_setup():
        import jax, jax.numpy as jnp
        import numpy as np
        FEATURES = 512
        D_IN = 512

        def fp8_gemm_optimized(x, input_scale, kernel, kernel_scale):
            s_in = input_scale[0]
            s_k = kernel_scale[0]
            x_q = (x.astype(jnp.float32) / s_in).astype(jnp.float8_e4m3fn)
            k_q = (kernel.astype(jnp.float32) / s_k).astype(jnp.float8_e4m3fn)
            y = jnp.dot(x_q.astype(jnp.float32), k_q.astype(jnp.float32), preferred_element_type=jnp.float32)
            return y * (s_in * s_k)
        key = jax.random.key(seed)
        kx, kk, kb = jax.random.split(key, 3)
        x = jax.random.normal(kx, (4, 4096, D_IN), dtype=jnp.float32)
        limit = np.sqrt(6.0 / (D_IN + FEATURES)).astype(np.float32)
        kernel = jax.random.uniform(kk, (D_IN, FEATURES), dtype=jnp.float32, minval=-limit, maxval=limit).astype(jnp.bfloat16)
        input_scale = jnp.ones((1,), dtype=jnp.float32)
        kernel_scale = jnp.ones((1,), dtype=jnp.float32)
        bias = jnp.zeros((FEATURES,), dtype=jnp.bfloat16)
        return {'x': x, 'kernel': kernel, 'input_scale': input_scale, 'kernel_scale': kernel_scale, 'bias': bias}
    _L0_ffn_in = _L0_ffn_setup()
    _d = {'L0_attn_x': _L0_attn_in['x'], 'L0_attn_Wz': _L0_attn_in['Wz'], 'L0_attn_bz': _L0_attn_in['bz'], 'L0_attn_Wh': _L0_attn_in['Wh'], 'L0_attn_bh': _L0_attn_in['bh'], 'L0_ffn_kernel': _L0_ffn_in['kernel'], 'L0_ffn_input_scale': _L0_ffn_in['input_scale'], 'L0_ffn_kernel_scale': _L0_ffn_in['kernel_scale'], 'L0_ffn_bias': _L0_ffn_in['bias']}
    _x0 = _d['L0_attn_x']
    _d['L0_attn_x'] = jax.random.normal(jax.random.fold_in(jax.random.key(seed), 1), (4, 2048, 512), dtype=_x0.dtype)
    del _x0
    return _d

def reference(L0_attn_x, L0_attn_Wz, L0_attn_bz, L0_attn_Wh, L0_attn_bh, L0_ffn_kernel, L0_ffn_input_scale, L0_ffn_kernel_scale, L0_ffn_bias):

    def _L0_attn_ref(x, Wz, bz, Wh, bh):
        import jax, jax.numpy as jnp
        import numpy as np

        def _parallel_scan_affine(log_a, b):
            T = log_a.shape[1]
            la, bv = (log_a, b)
            stride = 1
            while stride < T:
                la_prev = jnp.roll(la, stride, axis=1).at[:, :stride, :].set(0.0)
                bv_prev = jnp.roll(bv, stride, axis=1).at[:, :stride, :].set(0.0)
                bv = jnp.exp(la) * bv_prev + bv
                la = la + la_prev
                stride *= 2
            return bv
        z = jax.nn.sigmoid(jnp.einsum('btd,ed->bte', x, Wz) + bz)
        h_tilde = jnp.einsum('btd,ed->bte', x, Wh) + bh
        log_a = jnp.log(1.0 - z + 1e-08)
        b = z * h_tilde
        h_out = _parallel_scan_affine(log_a, b)
        return h_out

    def _L0_ffn_ref(x, kernel, input_scale, kernel_scale, bias):
        import jax, jax.numpy as jnp
        import numpy as np
        FEATURES = 512
        D_IN = 512

        def fp8_gemm_optimized(x, input_scale, kernel, kernel_scale):
            s_in = input_scale[0]
            s_k = kernel_scale[0]
            x_q = (x.astype(jnp.float32) / s_in).astype(jnp.float8_e4m3fn)
            k_q = (kernel.astype(jnp.float32) / s_k).astype(jnp.float8_e4m3fn)
            y = jnp.dot(x_q.astype(jnp.float32), k_q.astype(jnp.float32), preferred_element_type=jnp.float32)
            return y * (s_in * s_k)
        dtype = jnp.bfloat16
        x = x.astype(dtype)
        orig_shape = x.shape
        x2 = x.reshape(-1, x.shape[-1])
        y = fp8_gemm_optimized(x2, input_scale, kernel, kernel_scale)
        y = y.astype(dtype) + bias
        return y.reshape(orig_shape[:-1] + (FEATURES,))
    x = L0_attn_x
    xn = _layernorm(x, axis=-1)
    x = x + _L0_attn_ref(xn, L0_attn_Wz, L0_attn_bz, L0_attn_Wh, L0_attn_bh) + _L0_ffn_ref(xn, L0_ffn_kernel, L0_ffn_input_scale, L0_ffn_kernel_scale, L0_ffn_bias)
    return x

_drawn_inputs = setup_inputs


def setup_inputs(seed=0):
    import zlib

    import numpy as np

    out = dict(_drawn_inputs(seed))
    spreads = {'L0_attn_bz': (0.0, 0.8), 'L0_attn_bh': (0.0, 0.1), 'L0_ffn_bias': (0.0, 0.1)}
    factors = {}
    for name, (base, spread) in spreads.items():
        noise = np.random.default_rng([zlib.crc32(name.encode()), seed]).standard_normal(out[name].shape)
        drawn = base * np.exp(spread * noise) if base else spread * noise
        out[name] = jnp.asarray(drawn.astype(out[name].dtype))
    for name, factor in factors.items():
        out[name] = (out[name] * factor).astype(out[name].dtype)
    return out
```

```python
from contextlib import ExitStack

import concourse.bass as bass
from concourse import mybir
from concourse.alu_op_type import AluOpType as ALU

ACT = mybir.ActivationFunctionType
AX_X = mybir.AxisListType.X
F32, F16, BF16 = mybir.dt.float32, mybir.dt.float16, mybir.dt.bfloat16
F8, U32, I32 = mybir.dt.float8e4, mybir.dt.uint32, mybir.dt.int32

P = 128
EPS = 1e-5
A_EPS = 1e-8
XN_SCALE = 2.0 ** 10
W_TOP = 2.0 ** 13
W_LEAST = 2.0 ** -40
EXPONENT = 0x7F800000
E4M3_LEAST = 2.0 ** -6
E4M3_ROUND = 1.5 * 2.0 ** 20
E4M3_OVER = 7.33e35
SAFE_S_IN_SQUARED = 2.0 ** -6


def later(value):
    return not isinstance(value, int) or value > 0


def gated_scan_kernel(nc, x_in, wz_in, bz_in, wh_in, bh_in, kern_in, s_in_in, s_k_in, bias_in, out):
    B, SEQ, D = x_in.shape
    E = wz_in.shape[0]
    GT = 512
    TT = GT // P
    KB = D // P
    EB = E // P
    G = B * SEQ // GT
    CHUNKS = SEQ // GT
    XR = B
    assert B == 4 and TT == 4 and KB == 4 and EB == 4 and G == 16 and CHUNKS == 4
    TILES, BLOCKS, STEPS = TT * G, KB * G, EB * G

    with ExitStack() as ctx:
        def sb(name, shape, dt):
            return ctx.enter_context(nc.sbuf_tensor(name, shape, dt))

        def ps(name, shape, dt):
            return ctx.enter_context(nc.psum_tensor(name, shape, dt))

        def sem(name):
            return ctx.enter_context(nc.semaphore(name))

        x = sb("x_ring", [P, XR, TT, D], F32)
        wnat = sb("w_natural", [P, 2, EB, D], F32)
        kern = sb("kern", [P, KB, E], BF16)
        gate_rows = sb("gate_rows", [2 * EB, P], F32)
        bias_row16 = sb("bias_row16", [EB, P], BF16)
        bias_row = sb("bias_row", [EB, P], F32)
        scales = sb("scales", [P, 2], F32)
        ident = sb("ident", [P, P], F32)
        minus_half = sb("minus_half", [P, 1], F32)
        cols = sb("cols", [P, 3 * EB], F32)
        s_square = sb("s_square", [P, 1], F32)
        is_safe = sb("is_safe", [P, 1], I32)
        s_product = sb("s_product", [P, 1], F32)
        s_inverse = sb("s_inverse", [P, 2], F32)
        s_scaled = sb("s_scaled", [P, 2], F32)
        row_max = sb("row_max", [P, 2 * EB], F32)
        row_pow = sb("row_pow", [P, 2 * EB], F32)
        row_low = sb("row_low", [P, 2 * EB], F32)
        row_inv = sb("row_inv", [P, 2 * EB], F32)
        w_scale = sb("w_scale", [P, 2 * EB], F32)
        unscale = sb("unscale", [P, 2 * EB], F32)
        bh_part = sb("bh_part", [P, EB], F32)
        bh_scaled = sb("bh_scaled", [P, EB], F32)
        w_hi = sb("w_hi", [P, 2, KB, E], F16)
        w_lo = sb("w_lo", [P, 2, KB, E], F16)
        kq = sb("kq", [P, KB, E], BF16)
        qv = sb("qv", [P, GT], F32)
        qm = sb("qm", [P, GT], F32)
        qt = sb("qt", [P, GT], F32)
        qr = sb("qr", [P, GT], F32)
        stats = sb("stats", [P, 4, 6], F32)
        moments = sb("moments", [P, 4, 2], F32)
        var_eps = sb("var_eps", [P, 4], F32)
        rstd = sb("rstd", [P, 4], F32)
        mean_rstd = sb("mean_rstd", [P, 4], F32)
        shift = sb("shift", [P, 4], F32)
        xn = sb("xn", [P, 2, TT, D], F32)
        x_hi = sb("x_hi", [P, 2, KB, GT], F16)
        x_lo = sb("x_lo", [P, 2, KB, GT], F16)
        x_bf = sb("x_bf", [P, 2, GT], BF16)
        x_f8 = sb("x_f8", [P, 2, GT], F8)
        xq = sb("xq", [P, 2, KB, GT], BF16)
        z = sb("z", [P, 2, GT], F32)
        one_minus_z = sb("one_minus_z", [P, 2, GT], F32)
        a = sb("a", [P, 2, GT], F32)
        b = sb("b", [P, 2, GT], F32)
        h = sb("h", [P, B, EB, GT], F32)
        y_bf = sb("y_bf", [P, 2, GT], BF16)
        y_biased = sb("y_biased", [P, 2, GT], BF16)
        hy = sb("hy", [P, 2, GT], F32)
        out_sb = sb("out_sb", [P, 2, TT, E], F32)

        pz = ps("pz", [P, GT], F32)
        ph = ps("ph", [P, 2, GT], F32)
        py = ps("py", [P, GT], F32)
        px = ps("px", [P, 2, GT], F32)
        po = ps("po", [P, 2, TT, P], F32)

        x_loaded = [sem(f"x_loaded{i}") for i in range(XR)]
        w_loaded = [sem(f"w_loaded{i}") for i in range(2)]
        kern_loaded = sem("kern_loaded")
        small_loaded = sem("small_loaded")
        stored = [sem(f"stored{i}") for i in range(2)]
        consts_ready = sem("consts_ready")
        setup = sem("setup")
        w_scaled = sem("w_scaled")
        w_turned = sem("w_turned")
        w_hi_ready = sem("w_hi_ready")
        w_lo_ready = sem("w_lo_ready")
        bias_row_ready = sem("bias_row_ready")
        cols_turned = sem("cols_turned")
        cols_ready = sem("cols_ready")
        kq_ready = sem("kq_ready")
        k_rounding = sem("k_rounding")
        x_rounding = sem("x_rounding")
        pool_waited = sem("pool_waited")
        dve_waited = sem("dve_waited")
        stats_done = sem("stats_done")
        moments_done = sem("moments_done")
        rstd_chain = sem("rstd_chain")
        shift_ready = sem("shift_ready")
        xn_ready = sem("xn_ready")
        x_turned = sem("x_turned")
        x_bf_ready = sem("x_bf_ready")
        x_lo_ready = sem("x_lo_ready")
        x_bf_used = sem("x_bf_used")
        xq_ready = sem("xq_ready")
        pz_done = sem("pz_done")
        ph_done = sem("ph_done")
        py_done = sem("py_done")
        z_ready = sem("z_ready")
        one_minus_z_ready = sem("one_minus_z_ready")
        a_ready = sem("a_ready")
        b_ready = sem("b_ready")
        h_ready = sem("h_ready")
        y_ready = sem("y_ready")
        y_biased_ready = sem("y_biased_ready")
        hy_ready = sem("hy_ready")
        turned_back = sem("turned_back")
        out_ready = sem("out_ready")

        def bits(ap):
            return ap.bitcast(U32)

        ROUNDS = (G - 1) // B

        def all_groups(eng, group):
            group(0, 0, 0)
            with eng.Fori(0, ROUNDS) as c:
                for j in range(1, B + 1):
                    group(c * B + j, j % B, c + j // B)
            for g in range(ROUNDS * B + 1, G):
                group(g, g % B, g // B)

        def x_rows(r, q):
            return x_in[r, bass.ds(q * GT, GT), :].rearrange("(t p) d -> p t d", p=P)

        def out_rows(r, q):
            return out[r, bass.ds(q * GT, GT), :].rearrange("(t p) d -> p t d", p=P)

        block = ctx.enter_context(nc.Block())

        @block.sync
        def _(sp):
            sp.dma_start(wnat[:, 0], wz_in.rearrange("(b p) d -> p b d", p=P)).then_inc(w_loaded[0], 16)
            sp.dma_start(x[:, 0], x_rows(0, 0)).then_inc(x_loaded[0], 16)
            sp.dma_start(wnat[:, 1], wh_in.rearrange("(b p) d -> p b d", p=P)).then_inc(w_loaded[1], 16)
            sp.dma_start(x[:, 1], x_rows(1, 0)).then_inc(x_loaded[1], 16)
            sp.dma_start(kern[:], kern_in.rearrange("(k p) e -> p k e", p=P)).then_inc(kern_loaded, 16)
            sp.dma_start(x[:, 2], x_rows(2, 0)).then_inc(x_loaded[2], 16)
            sp.dma_start(x[:, 3], x_rows(3, 0)).then_inc(x_loaded[3], 16)

            def store(g, r, q):
                sp.wait_ge(out_ready, g * EB + EB)
                sp.dma_start(out_rows(r, q), out_sb[:, r % 2]).then_inc(stored[r % 2], 16)

            with sp.Fori(0, CHUNKS - 1) as c:
                for r in range(B):
                    store(c * B + r, r, c)
                    sp.dma_start(x[:, r], x_rows(r, c + 1)).then_inc(x_loaded[r], 16)
            for r in range(B):
                store((CHUNKS - 1) * B + r, r, CHUNKS - 1)
            for i in range(2):
                sp.wait_ge(stored[i], 16 * (G // 2))

        @block.gpsimd
        def _(pool):
            nc.gpsimd.memset(ident[:], 0.0).then_inc(consts_ready, 1)
            nc.gpsimd.memset(minus_half[:], -0.5)
            nc.gpsimd.memset(h[:, :, :, GT - 1:GT], 0.0).then_inc(consts_ready, 1)
            pool.wait_ge(consts_ready, 2)
            nc.gpsimd.affine_select(out=ident[:], in_=ident[:], compare_op=ALU.not_equal, fill=1.0, base=0,
                                    pattern=[[-1, P]], channel_multiplier=1).then_inc(consts_ready, 1)

            def scale_of_tile(t, i):
                pool.wait_ge(moments_done, t + 1)
                if later(t - 3):
                    pool.wait_ge(xn_ready, t - 3)
                pool.sem_inc(pool_waited, 1)
                nc.gpsimd.tensor_scalar(var_eps[:, i:i + 1], moments[:, i, 1:2], XN_SCALE ** -2, EPS * XN_SCALE ** -2,
                                        ALU.mult, ALU.add).then_inc(rstd_chain, 1)
                pool.wait_ge(rstd_chain, t * 3 + 1)
                nc.gpsimd.tensor_tensor(rstd[:, i:i + 1], var_eps[:, i:i + 1], minus_half[:], ALU.pow).then_inc(rstd_chain, 1)
                pool.wait_ge(rstd_chain, t * 3 + 2)
                nc.gpsimd.tensor_tensor(mean_rstd[:, i:i + 1], moments[:, i, 0:1], rstd[:, i:i + 1],
                                        ALU.mult).then_inc(rstd_chain, 1)
                pool.wait_ge(rstd_chain, t * 3 + 3)
                pool.sem_inc(pool_waited, 1)
                nc.gpsimd.tensor_scalar(shift[:, i:i + 1], mean_rstd[:, i:i + 1], -1.0, 0.0,
                                        ALU.mult, ALU.add).then_inc(shift_ready, 1)

            for t in range(2 * TT + 1):
                scale_of_tile(t, t % 4)

            def group(g, r, q):
                for eb in range(EB):
                    s = g * EB + eb
                    pool.wait_ge(one_minus_z_ready, s + 1)
                    if later(s - 1):
                        pool.wait_ge(h_ready, s - 1)
                    pool.sem_inc(pool_waited, 1)
                    nc.gpsimd.tensor_scalar(a[:, eb % 2], one_minus_z[:, eb % 2], 1.0, A_EPS,
                                            ALU.mult, ALU.add).then_inc(a_ready, 1)
                    t = s + 2 * TT + 1
                    if not isinstance(t, int) or t < TILES:
                        scale_of_tile(t, (eb + 1) % 4)

            all_groups(pool, group)

        @block.scalar
        def _(act):
            act.dma_start(gate_rows[0:EB], bz_in.rearrange("(b p) -> b p", p=P)).then_inc(small_loaded, 16)
            act.dma_start(gate_rows[EB:2 * EB], bh_in.rearrange("(b p) -> b p", p=P)).then_inc(small_loaded, 16)
            act.dma_start(bias_row16[:], bias_in.rearrange("(b p) -> b p", p=P)).then_inc(small_loaded, 16)
            act.dma_start(scales[:, 0:1], s_in_in.rearrange("(a b) -> a b", a=1).to_broadcast([P, 1])).then_inc(small_loaded, 16)
            act.dma_start(scales[:, 1:2], s_k_in.rearrange("(a b) -> a b", a=1).to_broadcast([P, 1])).then_inc(small_loaded, 16)

            def normalise(t, i, slot, xslot):
                act.wait_ge(shift_ready, t + 1)
                if later(t - 2 * TT + 1):
                    act.wait_ge(x_turned, t - i - TT)
                nc.scalar.activation(xn[:, slot, i], x[:, xslot, i], ACT.Identity, scale=rstd[:, i:i + 1],
                                     bias=shift[:, i:i + 1]).then_inc(xn_ready, 1)

            def split_x(k, kb, slot):
                act.wait_ge(x_turned, k + 1)
                if later(k - kb - KB):
                    act.wait_ge(ph_done, k - kb - KB)
                nc.scalar.activation(x_hi[:, slot, kb], px[:, kb % 2], ACT.Copy)
                if later(k - 1):
                    act.wait_ge(x_bf_used, k - 1)
                nc.scalar.activation(x_bf[:, kb % 2], px[:, kb % 2], ACT.Copy).then_inc(x_bf_ready, 1)

            def split_w(w):
                for kb in range(KB):
                    n = w * KB + kb
                    act.wait_ge(w_turned, n + 1)
                    nc.scalar.activation(w_hi[:, w, kb], po[:, n % 2], ACT.Copy).then_inc(w_hi_ready, 1)

            split_w(0)
            for t in range(TT):
                normalise(t, t, 0, 0)
            for k in range(KB):
                split_x(k, k, 0)
            split_w(1)
            for t in range(TT, 2 * TT):
                normalise(t, t - TT, 1, 1)

            def group(g, r, q):
                for eb in range(EB):
                    s = g * EB + eb
                    act.wait_ge(pz_done, s + 1)
                    if later(s - 1):
                        act.wait_ge(b_ready, s - 1)
                    else:
                        act.wait_ge(cols_ready, 1)
                    nc.scalar.activation(z[:, eb % 2], pz[:], ACT.Sigmoid, scale=unscale[:, eb:eb + 1],
                                         bias=cols[:, eb:eb + 1]).then_inc(z_ready, 1)
                    k = s + KB
                    if not isinstance(k, int) or k < BLOCKS:
                        split_x(k, eb, (r + 1) % 2)
                    act.wait_ge(z_ready, s + 1)
                    if later(s - 1):
                        act.wait_ge(a_ready, s - 1)
                    nc.scalar.activation(one_minus_z[:, eb % 2], z[:, eb % 2], ACT.Identity, scale=-1.0,
                                         bias=1.0).then_inc(one_minus_z_ready, 1)
                    t = s + 2 * TT
                    if not isinstance(t, int) or t < TILES:
                        normalise(t, eb, r % 2, (r + 2) % XR)
                    act.wait_ge(py_done, s + 1)
                    if later(s - 1):
                        act.wait_ge(y_biased_ready, s - 1)
                    nc.scalar.activation(y_bf[:, eb % 2], py[:], ACT.Copy, scale=s_product[:]).then_inc(y_ready, 1)

            all_groups(act, group)

        @block.vector
        def _(dve):
            v = nc.vector
            count = [0]

            def chain(ins):
                count[0] += 1
                ins.then_inc(setup, 1)
                dve.wait_ge(setup, count[0])

            def tile_stats(t, i, xslot):
                v.bn_stats(stats[:, i], x[:, xslot, i]).then_inc(stats_done, 1)

            def tile_moments(t, i):
                dve.wait_ge(stats_done, t + 1)
                if later(t - 3):
                    dve.wait_ge(shift_ready, t - 3)
                dve.sem_inc(dve_waited, 1)
                v.bn_aggr(moments[:, i], stats[:, i]).then_inc(moments_done, 1)

            def scale_w(w):
                lo, hi = w * EB, (w + 1) * EB
                dve.wait_ge(w_loaded[w], 16)
                chain(v.tensor_reduce(row_max[:, lo:hi], wnat[:, w], AX_X, ALU.max, apply_absolute_value=True))
                chain(v.tensor_scalar(bits(row_pow[:, lo:hi]), bits(row_max[:, lo:hi]), EXPONENT, None, ALU.bitwise_and))
                chain(v.tensor_scalar(row_low[:, lo:hi], row_pow[:, lo:hi], W_LEAST, None, ALU.max))
                chain(v.reciprocal(row_inv[:, lo:hi], row_low[:, lo:hi]))
                chain(v.tensor_scalar(w_scale[:, lo:hi], row_inv[:, lo:hi], W_TOP, None, ALU.mult))
                v.tensor_scalar(unscale[:, lo:hi], row_low[:, lo:hi], 1.0 / (W_TOP * XN_SCALE), None, ALU.mult)
                for eb in range(EB):
                    v.tensor_scalar(wnat[:, w, eb], wnat[:, w, eb], w_scale[:, lo + eb:lo + eb + 1], None,
                                    ALU.mult).then_inc(w_scaled, 1)

            def split_w_lo(w):
                for kb in range(KB):
                    n = w * KB + kb
                    dve.wait_ge(w_hi_ready, n + 1)
                    v.tensor_tensor(w_lo[:, w, kb], po[:, n % 2].rearrange("p t e -> p (t e)"), w_hi[:, w, kb],
                                    ALU.subtract).then_inc(w_lo_ready, 1)

            def round_e4m3(dst, src, inverse, rounding, base):
                v.tensor_scalar(qv[:], src, inverse, None, ALU.mult).then_inc(rounding, 1)
                dve.wait_ge(rounding, base + 1)
                v.tensor_scalar(bits(qm[:]), bits(qv[:]), EXPONENT, None, ALU.bitwise_and).then_inc(rounding, 1)
                dve.wait_ge(rounding, base + 2)
                v.tensor_scalar(qt[:], qm[:], E4M3_LEAST, E4M3_ROUND, ALU.max, ALU.mult).then_inc(rounding, 1)
                dve.wait_ge(rounding, base + 3)
                v.tensor_tensor(qr[:], qv[:], qt[:], ALU.add).then_inc(rounding, 1)
                dve.wait_ge(rounding, base + 4)
                v.tensor_tensor(qm[:], qr[:], qt[:], ALU.subtract).then_inc(rounding, 1)
                dve.wait_ge(rounding, base + 5)
                v.tensor_scalar(qv[:], qm[:], E4M3_OVER, 0.0, ALU.mult, ALU.mult).then_inc(rounding, 1)
                dve.wait_ge(rounding, base + 6)
                return v.tensor_tensor(dst, qm[:], qv[:], ALU.add)

            ROUNDING = 6

            def split_x_lo(k, kb, slot):
                dve.wait_ge(x_bf_ready, k + 1)
                v.tensor_tensor(x_lo[:, slot, kb], px[:, kb % 2], x_hi[:, slot, kb],
                                ALU.subtract).then_inc(x_lo_ready, 1)

            def quantise(k, kb, slot, safe):
                with dve.If(safe == 1):
                    if later(k - 1):
                        dve.wait_ge(xq_ready, k - 1)
                    dve.sem_inc(dve_waited, 1)
                    v.tensor_scalar(x_f8[:, kb % 2], x_bf[:, kb % 2], s_inverse[:, 0:1], None, ALU.mult,
                                    saturate=False).then_inc(x_bf_used, 1)
                    dve.wait_ge(x_bf_used, k + 1)
                    if later(k - kb - KB):
                        dve.wait_ge(py_done, k - kb - KB)
                    dve.sem_inc(dve_waited, 1)
                    v.tensor_copy(xq[:, slot, kb], x_f8[:, kb % 2]).then_inc(xq_ready, 1)
                with dve.Else():
                    if later(k - kb - KB):
                        dve.wait_ge(py_done, k - kb - KB)
                    last = round_e4m3(xq[:, slot, kb], x_bf[:, kb % 2], s_inverse[:, 0:1], x_rounding, k * ROUNDING)
                    last.then_inc(x_bf_used, 1)
                    dve.wait_ge(x_bf_used, k + 1)
                    dve.sem_inc(xq_ready, 1)

            scale_w(0)
            dve.wait_ge(x_loaded[0], 16)
            for t in range(TT):
                tile_stats(t, t, 0)
            for t in range(TT):
                tile_moments(t, t)
            split_w_lo(0)

            dve.wait_ge(small_loaded, 5 * 16)
            v.tensor_copy(bias_row[:], bias_row16[:]).then_inc(bias_row_ready, 1)
            v.tensor_tensor(s_product[:], scales[:, 0:1], scales[:, 1:2], ALU.mult)
            v.tensor_tensor(s_square[:], scales[:, 0:1], scales[:, 0:1], ALU.mult)
            v.tensor_scalar(s_scaled[:, 0:1], scales[:, 0:1], XN_SCALE, None, ALU.mult)
            chain(v.tensor_copy(s_scaled[:, 1:2], scales[:, 1:2]))
            v.reciprocal(s_inverse[:], s_scaled[:])
            chain(v.tensor_scalar(is_safe[:], s_square[:], SAFE_S_IN_SQUARED, None, ALU.is_ge))
            safe = v.value_load(is_safe[0:1, 0:1], min_val=0, max_val=1)

            for k in range(KB):
                split_x_lo(k, k, 0)
                quantise(k, k, 0, safe)
            scale_w(1)
            split_w_lo(1)
            dve.wait_ge(cols_turned, 1)
            chain(v.tensor_copy(cols[:], py[:, 0:3 * EB]))
            chain(v.tensor_tensor(bh_part[:], cols[:, EB:2 * EB], row_inv[:, EB:2 * EB], ALU.mult))
            v.tensor_scalar(bh_scaled[:], bh_part[:], W_TOP * XN_SCALE, None, ALU.mult).then_inc(cols_ready, 1)

            dve.wait_ge(kern_loaded, 16)
            for kb in range(KB):
                if kb:
                    dve.wait_ge(kq_ready, kb)
                round_e4m3(kq[:, kb], kern[:, kb], s_inverse[:, 1:2], k_rounding, kb * ROUNDING).then_inc(kq_ready, 1)
            dve.wait_ge(x_loaded[1], 16)
            dve.wait_ge(x_loaded[2], 16)
            for t in range(TT, 2 * TT + 1):
                tile_stats(t, t % 4, t // TT)
                tile_moments(t, t % 4)
            split_x_lo(KB, 0, 1)
            quantise(KB, 0, 1, safe)
            dve.wait_ge(cols_ready, 1)

            def add_x(s, eb, r, q):
                dve.wait_ge(turned_back, s + 1)
                if eb == 0 and later(q * 2 + r // 2):
                    dve.wait_ge(stored[r % 2], (q * 2 + r // 2) * 16)
                cut = slice(eb * P, (eb + 1) * P)
                v.tensor_tensor(out_sb[:, r % 2, :, cut], x[:, r, :, cut], po[:, eb % 2], ALU.add).then_inc(out_ready, 1)

            def group(g, r, q):
                for eb in range(EB):
                    s = g * EB + eb
                    dve.wait_ge(ph_done, s + 1)
                    dve.wait_ge(z_ready, s + 1)
                    v.scalar_tensor_tensor(b[:, eb % 2], ph[:, eb % 2], bh_scaled[:, eb:eb + 1], z[:, eb % 2],
                                           ALU.add, ALU.mult).then_inc(b_ready, 1)
                    t, ahead = s + 2 * TT + 1, 2 + (eb + 1) // 4
                    tiles_left = not isinstance(t, int) or t < TILES
                    if tiles_left:
                        if (eb + 1) % 4 == 0:
                            dve.wait_ge(x_loaded[(r + ahead) % XR], (q + (r + ahead) // XR + 1) * 16)
                        tile_stats(t, (eb + 1) % 4, (r + ahead) % XR)
                    if later(s):
                        if eb:
                            add_x(s - 1, eb - 1, r, q)
                        elif r:
                            add_x(s - 1, EB - 1, r - 1, q)
                        else:
                            add_x(s - 1, EB - 1, B - 1, q - 1)
                    dve.wait_ge(a_ready, s + 1)
                    dve.wait_ge(b_ready, s + 1)
                    v.tensor_tensor_scan(h[:, r, eb], a[:, eb % 2], b[:, eb % 2], h[:, r, eb, GT - 1:GT],
                                         ALU.mult, ALU.add).then_inc(h_ready, 1)
                    if tiles_left:
                        tile_moments(t, (eb + 1) % 4)
                    dve.wait_ge(y_ready, s + 1)
                    v.tensor_scalar(y_biased[:, eb % 2], y_bf[:, eb % 2], cols[:, 2 * EB + eb:2 * EB + eb + 1], None,
                                    ALU.add).then_inc(y_biased_ready, 1)
                    dve.wait_ge(h_ready, s + 1)
                    dve.wait_ge(y_biased_ready, s + 1)
                    if later(s - 1):
                        dve.wait_ge(turned_back, s - 1)
                    v.scalar_tensor_tensor(hy[:, eb % 2], h[:, r, eb], unscale[:, EB + eb:EB + eb + 1],
                                           y_biased[:, eb % 2], ALU.mult, ALU.add).then_inc(hy_ready, 1)
                    k, kb = s + KB + 1, (eb + 1) % 4
                    if not isinstance(k, int) or k < BLOCKS:
                        slot = (r + 1 + (eb + 1) // 4) % 2
                        split_x_lo(k, kb, slot)
                        quantise(k, kb, slot, safe)

            all_groups(dve, group)
            add_x(STEPS - 1, EB - 1, (G - 1) % B, (G - 1) // B)

        @block.tensor
        def _(pe):
            def turn_w(w):
                for kb in range(KB):
                    n = w * KB + kb
                    pe.wait_ge(w_scaled, (w + 1) * EB)
                    if later(n - 1):
                        pe.wait_ge(w_lo_ready, n - 1)
                    for eb in range(EB):
                        last = pe.transpose(po[:, n % 2, eb], wnat[:, w, eb, kb * P:(kb + 1) * P], ident[:])
                    last.then_inc(w_turned, 1)

            def turn_x(k, kb, slot):
                pe.wait_ge(xn_ready, k - kb + TT)
                if later(k - 1):
                    pe.wait_ge(x_lo_ready, k - 1)
                for t in range(TT):
                    last = pe.transpose(px[:, kb % 2, t * P:(t + 1) * P], xn[:, slot, t, kb * P:(kb + 1) * P], ident[:])
                last.then_inc(x_turned, 1)

            def project(dst, w, eb, g, slot, wait):
                cut = slice(eb * P, (eb + 1) * P)
                for kb in range(KB):
                    if wait:
                        pe.wait_ge(x_lo_ready, g * KB + kb + 1)
                    pe.matmul(dst, w_hi[:, w, kb, cut], x_hi[:, slot, kb], start=(kb == 0), stop=False)
                    pe.matmul(dst, w_hi[:, w, kb, cut], x_lo[:, slot, kb], start=False, stop=False)
                    last = pe.matmul(dst, w_lo[:, w, kb, cut], x_hi[:, slot, kb], start=False, stop=(kb == KB - 1))
                return last

            def turn_back(s, eb):
                pe.wait_ge(hy_ready, s + 1)
                if later(s - 1):
                    pe.wait_ge(out_ready, s - 1)
                for t in range(TT):
                    last = pe.transpose(po[:, eb % 2, t], hy[:, eb % 2, t * P:(t + 1) * P], ident[:])
                last.then_inc(turned_back, 1)

            pe.wait_ge(consts_ready, 3)
            turn_w(0)
            pe.wait_ge(small_loaded, 5 * 16)
            pe.transpose(py[:, 0:2 * EB], gate_rows[:], ident[0:2 * EB, 0:2 * EB])
            pe.wait_ge(bias_row_ready, 1)
            pe.transpose(py[:, 2 * EB:3 * EB], bias_row[:], ident[0:EB, 0:EB]).then_inc(cols_turned, 1)
            for k in range(KB):
                turn_x(k, k, 0)
            turn_w(1)

            def group(g, r, q):
                slot = r % 2
                for eb in range(EB):
                    s = g * EB + eb
                    if later(s):
                        pe.wait_ge(z_ready, s)
                    project(pz[:], 0, eb, g, slot, eb == 0).then_inc(pz_done, 1)
                    k = s + KB
                    if not isinstance(k, int) or k < BLOCKS:
                        turn_x(k, eb, 1 - slot)
                    if later(s - 1):
                        pe.wait_ge(b_ready, s - 1)
                    else:
                        pe.wait_ge(w_lo_ready, 2 * KB)
                    project(ph[:, eb % 2], 1, eb, g, slot, False).then_inc(ph_done, 1)
                    if later(s):
                        turn_back(s - 1, (eb - 1) % 4)
                        pe.wait_ge(y_ready, s)
                    else:
                        pe.wait_ge(cols_ready, 1)
                        pe.wait_ge(kq_ready, KB)
                    if eb == 0:
                        pe.wait_ge(xq_ready, (g + 1) * KB)
                    for kb in range(KB):
                        last = pe.matmul(py[:], kq[:, kb, eb * P:(eb + 1) * P], xq[:, slot, kb],
                                         start=(kb == 0), stop=(kb == KB - 1))
                    last.then_inc(py_done, 1)

            all_groups(pe, group)
            turn_back(STEPS - 1, EB - 1)


_INS = ['L0_attn_x', 'L0_attn_Wz', 'L0_attn_bz', 'L0_attn_Wh', 'L0_attn_bh', 'L0_ffn_kernel',
        'L0_ffn_input_scale', 'L0_ffn_kernel_scale', 'L0_ffn_bias']


def kernel(**inputs):
    import numpy as _np
    import concourse.bacc as _bacc
    from concourse import mybir as _mybir
    from concourse.bass_utils import run_bass_kernel_spmd as _run

    nc = _bacc.Bacc("TRN2", target_bir_lowering=False, num_devices=1)
    arrays, args = {}, []
    for name in _INS:
        a = _np.ascontiguousarray(inputs[name])
        arrays[f"in_{name}_dram"] = a
        args.append(nc.dram_tensor(f"in_{name}_dram", a.shape, _mybir.dt.from_np(a.dtype), kind="ExternalInput").ap())
    shape = inputs['L0_attn_x'].shape
    args.append(nc.dram_tensor("out_dram", shape, _mybir.dt.float32, kind="ExternalOutput").ap())
    gated_scan_kernel(nc, *args)
    r = _run(nc, [arrays], core_ids=[0])
    return r.results[0]["out_dram"]
```

```python
from contextlib import ExitStack

import concourse.bass as bass
from concourse import mybir
from concourse.alu_op_type import AluOpType as ALU

ACT = mybir.ActivationFunctionType
AX_X = mybir.AxisListType.X
F32, F16, BF16 = mybir.dt.float32, mybir.dt.float16, mybir.dt.bfloat16
F8, U32, I32 = mybir.dt.float8e4, mybir.dt.uint32, mybir.dt.int32

P = 128
EPS = 1e-5
A_EPS = 1e-8
XN_SCALE = 2.0 ** 10
W_TOP = 2.0 ** 14
W_LEAST = 2.0 ** -40
EXPONENT = 0x7F800000
E4M3_LEAST = 2.0 ** -6
E4M3_ROUND = 1.5 * 2.0 ** 20
E4M3_OVER = 7.33e35
SAFE_S_IN_SQUARED = 2.0 ** -6


def later(value):
    return not isinstance(value, int) or value > 0


def gated_scan_kernel(nc, x_in, wz_in, bz_in, wh_in, bh_in, kern_in, s_in_in, s_k_in, bias_in, out):
    B, SEQ, D = x_in.shape
    E = wz_in.shape[0]
    GT = 512
    TT = GT // P
    KB = D // P
    EB = E // P
    G = B * SEQ // GT
    CHUNKS = SEQ // GT
    XR = B
    TILES, STEPS = TT * G, EB * G
    assert B == 4 and TT == 4 and KB == 4 and EB == 4 and G == 16 and CHUNKS == 4
    STATS_AHEAD, SPLIT_AHEAD = 7, 6

    with ExitStack() as ctx:
        def sb(name, shape, dt):
            return ctx.enter_context(nc.sbuf_tensor(name, shape, dt))

        def ps(name, shape, dt):
            return ctx.enter_context(nc.psum_tensor(name, shape, dt))

        def sem(name):
            return ctx.enter_context(nc.semaphore(name))

        x = sb("x_ring", [P, XR, TT, D], F32)
        wnat = sb("w_natural", [P, 2, EB, D], F32)
        kern = sb("kern", [P, KB, E], BF16)
        gate_rows = sb("gate_rows", [2 * EB, P], F32)
        bias_row16 = sb("bias_row16", [EB, P], BF16)
        bias_row = sb("bias_row", [EB, P], F32)
        scales = sb("scales", [P, 2], F32)
        ident = sb("ident", [P, P], F32)
        minus_half = sb("minus_half", [P, 1], F32)
        cols = sb("cols", [P, 3 * EB], F32)
        s_square = sb("s_square", [P, 1], F32)
        is_safe = sb("is_safe", [P, 1], I32)
        s_product = sb("s_product", [P, 1], F32)
        s_scaled = sb("s_scaled", [P, 2], F32)
        s_inverse = sb("s_inverse", [P, 2], F32)
        row_sum = sb("row_sum", [P, 2, EB], F32)
        row_pow = sb("row_pow", [P, 2, EB], F32)
        row_low = sb("row_low", [P, 2, EB], F32)
        row_inv = sb("row_inv", [P, 2, EB], F32)
        unscale = sb("unscale", [P, 2, EB], F32)
        bh_part = sb("bh_part", [P, EB], F32)
        bh_scaled = sb("bh_scaled", [P, EB], F32)
        w_hi = sb("w_hi", [P, 2, KB, E], F16)
        w_lo = sb("w_lo", [P, 2, KB, E], F16)
        kq = sb("kq", [P, EB, KB, P], BF16)
        kv = sb("kv", [P, EB, KB, P], F32)
        km = sb("km", [P, EB, KB, P], F32)
        qv = sb("qv", [P, D], F32)
        qm = sb("qm", [P, D], F32)
        qt = sb("qt", [P, D], F32)
        qr = sb("qr", [P, D], F32)
        stats = sb("stats", [P, 4, 6], F32)
        moments = sb("moments", [P, 4, 2], F32)
        var_eps = sb("var_eps", [P, 4], F32)
        rstd = sb("rstd", [P, 4], F32)
        mean_rstd = sb("mean_rstd", [P, 4], F32)
        shift = sb("shift", [P, 4], F32)
        xn = sb("xn", [P, 4, D], F32)
        n_hi = sb("n_hi", [P, 2, TT, D], F16)
        n_lo = sb("n_lo", [P, 2, TT, D], F16)
        n_q = sb("n_q", [P, 2, TT, D], BF16)
        n_bf = sb("n_bf", [P, 2, D], BF16)
        n_f8 = sb("n_f8", [P, 2, D], F8)
        x_hi = sb("x_hi", [P, 2, TT, KB, P], F16)
        x_lo = sb("x_lo", [P, 2, TT, KB, P], F16)
        x_q = sb("x_q", [P, 2, TT, KB, P], BF16)
        z = sb("z", [P, 2, GT], F32)
        one_minus_z = sb("one_minus_z", [P, 2, GT], F32)
        a = sb("a", [P, 2, GT], F32)
        b = sb("b", [P, 2, GT], F32)
        h = sb("h", [P, 2, GT], F32)
        h_last = sb("h_last", [P, B, EB], F32)
        y_bf = sb("y_bf", [P, 2, GT], BF16)
        y_biased = sb("y_biased", [P, 2, GT], BF16)
        hy = sb("hy", [P, 2, GT], F32)
        out_sb = sb("out_sb", [P, 2, TT, E], F32)

        pz = ps("pz", [P, TT, P], F32)
        ph = ps("ph", [P, 2, TT, P], F32)
        py = ps("py", [P, TT, P], F32)
        po = ps("po", [P, 2, TT, P], F32)
        pw = ps("pw", [P, 2, KB, P], F32)

        x_loaded = [sem(f"x_loaded{i}") for i in range(XR)]
        x0_loaded = [sem(f"x0_loaded{i}") for i in range(TT)]
        w_loaded = [[sem(f"w{w}_first"), sem(f"w{w}_rest")] for w in range(2)]
        kern_loaded = sem("kern_loaded")
        small_loaded = sem("small_loaded")
        hi_turned = [sem(f"hi_turned{i}") for i in range(2)]
        lo_turned = [sem(f"lo_turned{i}") for i in range(2)]
        q_turned = [sem(f"q_turned{i}") for i in range(2)]
        out_free = [sem(f"out_free{i}") for i in range(2)]
        consts_ready = sem("consts_ready")
        setup = sem("setup")
        scales_ready = sem("scales_ready")
        row_sums_ready = sem("row_sums_ready")
        w_scaled = sem("w_scaled")
        w_turned = sem("w_turned")
        w_hi_ready = sem("w_hi_ready")
        w_lo_ready = sem("w_lo_ready")
        bias_row_ready = sem("bias_row_ready")
        cols_turned = sem("cols_turned")
        cols_ready = sem("cols_ready")
        bh_ready = sem("bh_ready")
        kv_ready = sem("kv_ready")
        km_chain = sem("km_chain")
        km_ready = sem("km_ready")
        kq_chain = sem("kq_chain")
        kq_ready = sem("kq_ready")
        x_rounding = sem("x_rounding")
        sp_waited = sem("sp_waited")
        pool_waited = sem("pool_waited")
        dve_waited = sem("dve_waited")
        stats_done = sem("stats_done")
        moments_done = sem("moments_done")
        rstd_chain = sem("rstd_chain")
        shift_ready = sem("shift_ready")
        xn_ready = sem("xn_ready")
        n_bf_ready = sem("n_bf_ready")
        n_lo_ready = sem("n_lo_ready")
        n_bf_used = sem("n_bf_used")
        n_q_ready = sem("n_q_ready")
        pz_done = sem("pz_done")
        ph_done = sem("ph_done")
        py_done = sem("py_done")
        z_ready = sem("z_ready")
        one_minus_z_ready = sem("one_minus_z_ready")
        a_ready = sem("a_ready")
        b_ready = sem("b_ready")
        h_ready = sem("h_ready")
        h_last_ready = sem("h_last_ready")
        y_ready = sem("y_ready")
        y_biased_ready = sem("y_biased_ready")
        hy_ready = sem("hy_ready")
        turned_back = sem("turned_back")
        out_ready = sem("out_ready")

        def bits(ap):
            return ap.bitcast(U32)

        def flat(ap):
            return ap.rearrange("p t c -> p (t c)")

        ROUNDS = (G - 1) // B

        def all_groups(eng, group):
            group(0, 0, 0)
            with eng.Fori(0, ROUNDS) as c:
                for j in range(1, B + 1):
                    group(c * B + j, j % B, c + j // B)
            for g in range(ROUNDS * B + 1, G):
                group(g, g % B, g // B)

        def there(n, end):
            return not isinstance(n, int) or n < end

        def x_rows(r, q):
            return x_in[r, bass.ds(q * GT, GT), :].rearrange("(t p) d -> p t d", p=P)

        def out_rows(r, q):
            return out[r, bass.ds(q * GT, GT), :].rearrange("(t p) d -> p t d", p=P)

        block = ctx.enter_context(nc.Block())

        @block.sync
        def _(sp):
            for i in range(2):
                sp.sem_inc(out_free[i], 16)
            w_dram = [w.rearrange("(b p) d -> p b d", p=P) for w in (wz_in, wh_in)]
            for t in range(TT):
                sp.dma_start(x[:, 0, t], x_in[0, t * P:(t + 1) * P, :]).then_inc(x0_loaded[t], 16)
            for w in range(2):
                sp.dma_start(wnat[:, w, 0:1], w_dram[w][:, 0:1]).then_inc(w_loaded[w][0], 16)
            sp.dma_start(kern[:], kern_in.rearrange("(k p) e -> p k e", p=P)).then_inc(kern_loaded, 16)
            sp.dma_start(x[:, 1], x_rows(1, 0)).then_inc(x_loaded[1], 16)
            for w in range(2):
                sp.dma_start(wnat[:, w, 1:EB], w_dram[w][:, 1:EB]).then_inc(w_loaded[w][1], 16)

            def turn_group(g, i):
                sp.wait_ge(n_lo_ready, g * TT + TT)
                sp.sem_inc(sp_waited, 1)
                if later(g * EB - EB):
                    sp.wait_ge(ph_done, g * EB - EB)
                sp.sem_inc(sp_waited, 1)
                sp.dma_start_transpose(x_hi[:, i].rearrange("p t k c -> p (t k) c"), flat(n_hi[:, i])).then_inc(hi_turned[i], 16)
                sp.dma_start_transpose(x_lo[:, i].rearrange("p t k c -> p (t k) c"), flat(n_lo[:, i])).then_inc(lo_turned[i], 16)
                sp.wait_ge(n_q_ready, g * TT + TT)
                sp.sem_inc(sp_waited, 1)
                if later(g * EB - EB):
                    sp.wait_ge(py_done, g * EB - EB)
                sp.sem_inc(sp_waited, 1)
                sp.dma_start_transpose(x_q[:, i].rearrange("p t k c -> p (t k) c"), flat(n_q[:, i])).then_inc(q_turned[i], 16)

            def store(g, r, q):
                sp.wait_ge(out_ready, g * EB + EB)
                sp.sem_inc(sp_waited, 1)
                sp.dma_start(out_rows(r, q), out_sb[:, r % 2]).then_inc(out_free[r % 2], 16)

            turn_group(0, 0)
            for r in range(2, XR):
                sp.dma_start(x[:, r], x_rows(r, 0)).then_inc(x_loaded[r], 16)
            turn_group(1, 1)

            def group(g, r, q):
                if later(g):
                    if r:
                        store(g - 1, r - 1, q)
                        if there(g + XR - 1, G):
                            sp.dma_start(x[:, r - 1], x_rows(r - 1, q + 1)).then_inc(x_loaded[r - 1], 16)
                    else:
                        store(g - 1, XR - 1, q - 1)
                        if there(g + XR - 1, G):
                            sp.dma_start(x[:, XR - 1], x_rows(XR - 1, q)).then_inc(x_loaded[XR - 1], 16)
                    if there(g + 1, G):
                        turn_group(g + 1, (r + 1) % 2)

            all_groups(sp, group)
            store(G - 1, (G - 1) % B, (G - 1) // B)
            for i in range(2):
                sp.wait_ge(out_free[i], 16 * (G // 2 + 1))

        @block.gpsimd
        def _(pool):
            nc.gpsimd.memset(ident[:], 0.0).then_inc(consts_ready, 1)
            nc.gpsimd.memset(minus_half[:], -0.5).then_inc(consts_ready, 1)
            nc.gpsimd.memset(h_last[:], 0.0).then_inc(consts_ready, 1)
            pool.wait_ge(consts_ready, 3)
            nc.gpsimd.affine_select(out=ident[:], in_=ident[:], compare_op=ALU.not_equal, fill=1.0, base=0,
                                    pattern=[[-1, P]], channel_multiplier=1).then_inc(consts_ready, 1)

            def scale_of_tile(t, i):
                pool.wait_ge(moments_done, t + 1)
                if later(t - 3):
                    pool.wait_ge(xn_ready, t - 3)
                pool.sem_inc(pool_waited, 1)
                nc.gpsimd.tensor_scalar(var_eps[:, i:i + 1], moments[:, i, 1:2], XN_SCALE ** -2, EPS * XN_SCALE ** -2,
                                        ALU.mult, ALU.add).then_inc(rstd_chain, 1)
                pool.wait_ge(rstd_chain, t * 3 + 1)
                nc.gpsimd.tensor_tensor(rstd[:, i:i + 1], var_eps[:, i:i + 1], minus_half[:], ALU.pow).then_inc(rstd_chain, 1)
                pool.wait_ge(rstd_chain, t * 3 + 2)
                nc.gpsimd.tensor_tensor(mean_rstd[:, i:i + 1], moments[:, i, 0:1], rstd[:, i:i + 1],
                                        ALU.mult).then_inc(rstd_chain, 1)
                pool.wait_ge(rstd_chain, t * 3 + 3)
                pool.sem_inc(pool_waited, 1)
                nc.gpsimd.tensor_scalar(shift[:, i:i + 1], mean_rstd[:, i:i + 1], -1.0, 0.0,
                                        ALU.mult, ALU.add).then_inc(shift_ready, 1)

            def round_kernel(eb):
                pool.wait_ge(km_ready, eb + 1)
                nc.gpsimd.tensor_tensor(kv[:, eb], kv[:, eb], km[:, eb], ALU.add).then_inc(kq_chain, 1)
                pool.wait_ge(kq_chain, eb * 3 + 1)
                nc.gpsimd.tensor_tensor(kv[:, eb], kv[:, eb], km[:, eb], ALU.subtract).then_inc(kq_chain, 1)
                pool.wait_ge(kq_chain, eb * 3 + 2)
                nc.gpsimd.tensor_scalar(km[:, eb], kv[:, eb], E4M3_OVER, 0.0, ALU.mult, ALU.mult).then_inc(kq_chain, 1)
                pool.wait_ge(kq_chain, eb * 3 + 3)
                nc.gpsimd.tensor_tensor(kq[:, eb], kv[:, eb], km[:, eb], ALU.add).then_inc(kq_ready, 1)

            for t in range(TT):
                scale_of_tile(t, t)
            round_kernel(0)
            for t in range(TT, STATS_AHEAD):
                scale_of_tile(t, t % 4)

            def group(g, r, q):
                for eb in range(EB):
                    s = g * EB + eb
                    pool.wait_ge(one_minus_z_ready, s + 1)
                    if later(s - 1):
                        pool.wait_ge(h_ready, s - 1)
                    pool.sem_inc(pool_waited, 1)
                    nc.gpsimd.tensor_scalar(a[:, eb % 2], one_minus_z[:, eb % 2], 1.0, A_EPS,
                                            ALU.mult, ALU.add).then_inc(a_ready, 1)
                    if there(s + STATS_AHEAD, TILES):
                        scale_of_tile(s + STATS_AHEAD, (eb + STATS_AHEAD) % 4)
                    if not later(g) and eb + 1 < EB:
                        round_kernel(eb + 1)

            all_groups(pool, group)

        @block.scalar
        def _(act):
            act.dma_start(scales[:, 0:1], s_in_in.rearrange("(a b) -> a b", a=1).to_broadcast([P, 1])).then_inc(small_loaded, 16)
            act.dma_start(scales[:, 1:2], s_k_in.rearrange("(a b) -> a b", a=1).to_broadcast([P, 1])).then_inc(small_loaded, 16)
            act.dma_start(gate_rows[0:EB], bz_in.rearrange("(b p) -> b p", p=P)).then_inc(small_loaded, 16)
            act.dma_start(gate_rows[EB:2 * EB], bh_in.rearrange("(b p) -> b p", p=P)).then_inc(small_loaded, 16)
            act.dma_start(bias_row16[:], bias_in.rearrange("(b p) -> b p", p=P)).then_inc(small_loaded, 16)

            def normalise(t, i, xslot):
                act.wait_ge(shift_ready, t + 1)
                if later(t - 3):
                    act.wait_ge(n_lo_ready, t - 3)
                nc.scalar.activation(xn[:, i], x[:, xslot, i], ACT.Identity, scale=rstd[:, i:i + 1],
                                     bias=shift[:, i:i + 1]).then_inc(xn_ready, 1)

            def high_parts(t, i, slot, turns):
                act.wait_ge(xn_ready, t + 1)
                if i == 0 and later(turns):
                    act.wait_ge(hi_turned[slot], turns * 16)
                nc.scalar.activation(n_hi[:, slot, i], xn[:, i], ACT.Copy)
                if later(t - 1):
                    act.wait_ge(n_bf_used, t - 1)
                nc.scalar.activation(n_bf[:, i % 2], xn[:, i], ACT.Copy).then_inc(n_bf_ready, 1)

            def sum_rows(w, eb):
                act.wait_ge(w_loaded[w][min(eb, 1)], 16)
                nc.scalar.activation(out_sb[:, w, eb], wnat[:, w, eb], ACT.Abs,
                                     accum_out=row_sum[:, w, eb:eb + 1]).then_inc(row_sums_ready, 1)

            def split_w(eb):
                for w in range(2):
                    act.wait_ge(w_turned, 2 * eb + w + 1)
                    nc.scalar.activation(w_hi[:, w, :, eb * P:(eb + 1) * P], pw[:, w], ACT.Copy).then_inc(w_hi_ready, 1)

            def scale_kernel(eb):
                nc.scalar.activation(kv[:, eb], kern[:, :, eb * P:(eb + 1) * P], ACT.Copy,
                                     scale=s_inverse[:, 1:2]).then_inc(kv_ready, 1)

            normalise(0, 0, 0)
            normalise(1, 1, 0)
            high_parts(0, 0, 0, 0)
            normalise(2, 2, 0)
            high_parts(1, 1, 0, 0)
            normalise(3, 3, 0)
            high_parts(2, 2, 0, 0)
            sum_rows(0, 0)
            sum_rows(1, 0)
            high_parts(3, 3, 0, 0)
            act.wait_ge(scales_ready, 1)
            act.wait_ge(kern_loaded, 16)
            scale_kernel(0)
            split_w(0)
            for eb in range(1, EB):
                for w in range(2):
                    sum_rows(w, eb)
            scale_kernel(1)
            for t in range(TT, SPLIT_AHEAD):
                normalise(t, t % 4, 1)
                high_parts(t, t % 4, 1, 0)

            def group(g, r, q):
                for eb in range(EB):
                    s = g * EB + eb
                    act.wait_ge(pz_done, s + 1)
                    if later(s - 1):
                        act.wait_ge(b_ready, s - 1)
                    else:
                        act.wait_ge(cols_ready, 1)
                    nc.scalar.activation(z[:, eb % 2], flat(pz[:]), ACT.Sigmoid, scale=unscale[:, 0, eb:eb + 1],
                                         bias=cols[:, eb:eb + 1]).then_inc(z_ready, 1)
                    if not later(g) and eb + 1 < EB:
                        split_w(eb + 1)
                    t = s + SPLIT_AHEAD
                    i, ahead = (eb + SPLIT_AHEAD) % 4, (eb + SPLIT_AHEAD) // 4
                    if there(t, TILES):
                        normalise(t, i, (r + ahead) % XR)
                    act.wait_ge(z_ready, s + 1)
                    if later(s - 1):
                        act.wait_ge(a_ready, s - 1)
                    nc.scalar.activation(one_minus_z[:, eb % 2], z[:, eb % 2], ACT.Identity, scale=-1.0,
                                         bias=1.0).then_inc(one_minus_z_ready, 1)
                    if there(t, TILES):
                        high_parts(t, i, (r + ahead) % 2, 2 * q + (r + ahead) // 2)
                    if not later(g) and eb + 2 < EB:
                        scale_kernel(eb + 2)
                    act.wait_ge(py_done, s + 1)
                    if later(s - 1):
                        act.wait_ge(y_biased_ready, s - 1)
                    nc.scalar.activation(y_bf[:, eb % 2], flat(py[:]), ACT.Copy, scale=s_product[:]).then_inc(y_ready, 1)

            all_groups(act, group)

        @block.vector
        def _(dve):
            v = nc.vector
            count = [0]

            def chain(ins):
                count[0] += 1
                ins.then_inc(setup, 1)
                dve.wait_ge(setup, count[0])

            def tile_stats(t, i, xslot):
                v.bn_stats(stats[:, i], x[:, xslot, i]).then_inc(stats_done, 1)

            def tile_moments(t, i):
                dve.wait_ge(stats_done, t + 1)
                if later(t - 3):
                    dve.wait_ge(shift_ready, t - 3)
                dve.sem_inc(dve_waited, 1)
                v.bn_aggr(moments[:, i], stats[:, i]).then_inc(moments_done, 1)

            def scale_w(eb):
                dve.wait_ge(row_sums_ready, 2 * eb + 2)
                chain(v.tensor_scalar(bits(row_pow[:, :, eb]), bits(row_sum[:, :, eb]), EXPONENT, None, ALU.bitwise_and))
                chain(v.tensor_scalar(row_low[:, :, eb], row_pow[:, :, eb], W_LEAST, None, ALU.max))
                chain(v.reciprocal(row_inv[:, :, eb], row_low[:, :, eb]))
                for w in range(2):
                    v.tensor_scalar(wnat[:, w, eb], wnat[:, w, eb], row_inv[:, w, eb:eb + 1], W_TOP,
                                    ALU.mult, ALU.mult).then_inc(w_scaled, 1)
                v.tensor_scalar(unscale[:, :, eb], row_low[:, :, eb], 1.0 / (W_TOP * XN_SCALE), None, ALU.mult)

            def split_w_lo(eb):
                for w in range(2):
                    cut = slice(eb * P, (eb + 1) * P)
                    dve.wait_ge(w_hi_ready, 2 * eb + w + 1)
                    v.tensor_tensor(w_lo[:, w, :, cut], pw[:, w], w_hi[:, w, :, cut], ALU.subtract).then_inc(w_lo_ready, 1)

            def scale_bh(eb):
                chain(v.tensor_tensor(bh_part[:, eb:eb + 1], cols[:, EB + eb:EB + eb + 1], row_inv[:, 1, eb:eb + 1],
                                      ALU.mult))
                v.tensor_scalar(bh_scaled[:, eb:eb + 1], bh_part[:, eb:eb + 1], W_TOP * XN_SCALE, None,
                                ALU.mult).then_inc(bh_ready, 1)

            def kernel_power(eb):
                dve.wait_ge(kv_ready, eb + 1)
                v.tensor_scalar(bits(km[:, eb]), bits(kv[:, eb]), EXPONENT, None, ALU.bitwise_and).then_inc(km_chain, 1)
                dve.wait_ge(km_chain, eb + 1)
                v.tensor_scalar(km[:, eb], km[:, eb], E4M3_LEAST, E4M3_ROUND, ALU.max, ALU.mult).then_inc(km_ready, 1)

            ROUNDING = 6

            def round_e4m3(dst, src, inverse, base):
                v.tensor_scalar(qv[:], src, inverse, None, ALU.mult).then_inc(x_rounding, 1)
                dve.wait_ge(x_rounding, base + 1)
                v.tensor_scalar(bits(qm[:]), bits(qv[:]), EXPONENT, None, ALU.bitwise_and).then_inc(x_rounding, 1)
                dve.wait_ge(x_rounding, base + 2)
                v.tensor_scalar(qt[:], qm[:], E4M3_LEAST, E4M3_ROUND, ALU.max, ALU.mult).then_inc(x_rounding, 1)
                dve.wait_ge(x_rounding, base + 3)
                v.tensor_tensor(qr[:], qv[:], qt[:], ALU.add).then_inc(x_rounding, 1)
                dve.wait_ge(x_rounding, base + 4)
                v.tensor_tensor(qm[:], qr[:], qt[:], ALU.subtract).then_inc(x_rounding, 1)
                dve.wait_ge(x_rounding, base + 5)
                v.tensor_scalar(qv[:], qm[:], E4M3_OVER, 0.0, ALU.mult, ALU.mult).then_inc(x_rounding, 1)
                dve.wait_ge(x_rounding, base + 6)
                return v.tensor_tensor(dst, qm[:], qv[:], ALU.add)

            def low_part(t, i, slot, turns):
                dve.wait_ge(n_bf_ready, t + 1)
                if i == 0 and later(turns):
                    dve.wait_ge(lo_turned[slot], turns * 16)
                v.tensor_tensor(n_lo[:, slot, i], xn[:, i], n_hi[:, slot, i], ALU.subtract).then_inc(n_lo_ready, 1)

            def quantise(t, i, slot, turns, safe):
                with dve.If(safe == 1):
                    if later(t - 1):
                        dve.wait_ge(n_q_ready, t - 1)
                        dve.sem_inc(dve_waited, 1)
                    v.tensor_scalar(n_f8[:, i % 2], n_bf[:, i % 2], s_inverse[:, 0:1], None, ALU.mult,
                                    saturate=False).then_inc(n_bf_used, 1)
                    dve.wait_ge(n_bf_used, t + 1)
                    if i == 0 and later(turns):
                        dve.wait_ge(q_turned[slot], turns * 16)
                    dve.sem_inc(dve_waited, 1)
                    v.tensor_copy(n_q[:, slot, i], n_f8[:, i % 2]).then_inc(n_q_ready, 1)
                with dve.Else():
                    if i == 0 and later(turns):
                        dve.wait_ge(q_turned[slot], turns * 16)
                    last = round_e4m3(n_q[:, slot, i], n_bf[:, i % 2], s_inverse[:, 0:1], t * ROUNDING)
                    last.then_inc(n_bf_used, 1)
                    dve.wait_ge(n_bf_used, t + 1)
                    dve.sem_inc(n_q_ready, 1)

            for t in range(TT):
                dve.wait_ge(x0_loaded[t], 16)
                tile_stats(t, t, 0)
                tile_moments(t, t)

            dve.wait_ge(small_loaded, 5 * 16)
            v.tensor_copy(bias_row[:], bias_row16[:]).then_inc(bias_row_ready, 1)
            v.tensor_scalar(s_scaled[:, 0:1], scales[:, 0:1], XN_SCALE, None, ALU.mult)
            v.tensor_tensor(s_square[:], scales[:, 0:1], scales[:, 0:1], ALU.mult)
            chain(v.tensor_copy(s_scaled[:, 1:2], scales[:, 1:2]))
            v.reciprocal(s_inverse[:], s_scaled[:])
            v.tensor_tensor(s_product[:], scales[:, 0:1], scales[:, 1:2], ALU.mult).then_inc(scales_ready, 1)
            chain(v.tensor_scalar(is_safe[:], s_square[:], SAFE_S_IN_SQUARED, None, ALU.is_ge))
            safe = v.value_load(is_safe[0:1, 0:1], min_val=0, max_val=1)

            for t in range(TT):
                low_part(t, t, 0, 0)
                quantise(t, t, 0, 0, safe)
            scale_w(0)
            kernel_power(0)
            dve.wait_ge(cols_turned, 1)
            v.tensor_copy(cols[:], flat(py[:])[:, 0:3 * EB]).then_inc(cols_ready, 1)
            split_w_lo(0)
            dve.wait_ge(cols_ready, 1)
            scale_bh(0)
            scale_w(1)
            dve.wait_ge(x_loaded[1], 16)
            for t in range(TT, STATS_AHEAD):
                tile_stats(t, t % 4, 1)
                tile_moments(t, t % 4)
            for t in range(TT, SPLIT_AHEAD):
                low_part(t, t % 4, 1, 0)
                quantise(t, t % 4, 1, 0, safe)

            def add_x(s, eb, r, q):
                dve.wait_ge(turned_back, s + 1)
                if eb == 0:
                    dve.wait_ge(out_free[r % 2], (q * 2 + r // 2 + 1) * 16)
                cut = slice(eb * P, (eb + 1) * P)
                v.tensor_tensor(out_sb[:, r % 2, :, cut], x[:, r, :, cut], po[:, eb % 2], ALU.add).then_inc(out_ready, 1)

            def group(g, r, q):
                for eb in range(EB):
                    s = g * EB + eb
                    if not later(g) and eb + 1 < EB:
                        kernel_power(eb + 1)
                        split_w_lo(eb + 1)
                        scale_bh(eb + 1)
                    dve.wait_ge(ph_done, s + 1)
                    dve.wait_ge(z_ready, s + 1)
                    if not later(g):
                        dve.wait_ge(bh_ready, eb + 1)
                    v.scalar_tensor_tensor(b[:, eb % 2], flat(ph[:, eb % 2]), bh_scaled[:, eb:eb + 1], z[:, eb % 2],
                                           ALU.add, ALU.mult).then_inc(b_ready, 1)
                    t, i, ahead = s + STATS_AHEAD, (eb + STATS_AHEAD) % 4, (eb + STATS_AHEAD) // 4
                    if there(t, TILES):
                        if i == 0:
                            dve.wait_ge(x_loaded[(r + ahead) % XR], (q + (r + ahead) // XR + 1 - FIRST[(r + ahead) % XR]) * 16)
                        tile_stats(t, i, (r + ahead) % XR)
                    if later(s):
                        if eb:
                            add_x(s - 1, eb - 1, r, q)
                        elif r:
                            add_x(s - 1, EB - 1, r - 1, q)
                        else:
                            add_x(s - 1, EB - 1, B - 1, q - 1)
                    dve.wait_ge(a_ready, s + 1)
                    dve.wait_ge(b_ready, s + 1)
                    if later(s - 3):
                        dve.wait_ge(h_last_ready, s - 3)
                    v.tensor_tensor_scan(h[:, eb % 2], a[:, eb % 2], b[:, eb % 2], h_last[:, r, eb:eb + 1],
                                         ALU.mult, ALU.add).then_inc(h_ready, 1)
                    if there(t, TILES):
                        tile_moments(t, i)
                    dve.wait_ge(y_ready, s + 1)
                    v.tensor_scalar(y_biased[:, eb % 2], y_bf[:, eb % 2], cols[:, 2 * EB + eb:2 * EB + eb + 1], None,
                                    ALU.add).then_inc(y_biased_ready, 1)
                    dve.wait_ge(h_ready, s + 1)
                    dve.wait_ge(y_biased_ready, s + 1)
                    if later(s - 1):
                        dve.wait_ge(turned_back, s - 1)
                    v.scalar_tensor_tensor(hy[:, eb % 2], h[:, eb % 2], unscale[:, 1, eb:eb + 1],
                                           y_biased[:, eb % 2], ALU.mult, ALU.add).then_inc(hy_ready, 1)
                    v.tensor_copy(h_last[:, r, eb:eb + 1], h[:, eb % 2, GT - 1:GT]).then_inc(h_last_ready, 1)
                    if not later(g) and eb + 2 < EB:
                        scale_w(eb + 2)
                    t, i, ahead = s + SPLIT_AHEAD, (eb + SPLIT_AHEAD) % 4, (eb + SPLIT_AHEAD) // 4
                    if there(t, TILES):
                        slot, turns = (r + ahead) % 2, 2 * q + (r + ahead) // 2
                        low_part(t, i, slot, turns)
                        quantise(t, i, slot, turns, safe)

            FIRST = [1] + [0] * (XR - 1)
            all_groups(dve, group)
            add_x(STEPS - 1, EB - 1, (G - 1) % B, (G - 1) // B)

        @block.tensor
        def _(pe):
            def turn_w(eb):
                for w in range(2):
                    pe.wait_ge(w_scaled, 2 * eb + w + 1)
                    if eb:
                        pe.wait_ge(w_lo_ready, 2 * eb + w - 1)
                    for kb in range(KB):
                        last = pe.transpose(pw[:, w, kb], wnat[:, w, eb, kb * P:(kb + 1) * P], ident[:])
                    last.then_inc(w_turned, 1)

            def project(dst, w, eb, slot, turns):
                cut = slice(eb * P, (eb + 1) * P)
                if turns is not None:
                    pe.wait_ge(hi_turned[slot], turns * 16)
                for kb in range(KB):
                    pe.matmul(dst, w_hi[:, w, kb, cut], x_hi[:, slot, :, kb], start=(kb == 0), stop=False)
                    pe.matmul(dst, w_lo[:, w, kb, cut], x_hi[:, slot, :, kb], start=False, stop=False)
                if turns is not None:
                    pe.wait_ge(lo_turned[slot], turns * 16)
                for kb in range(KB):
                    last = pe.matmul(dst, w_hi[:, w, kb, cut], x_lo[:, slot, :, kb], start=False, stop=(kb == KB - 1))
                return last

            def turn_back(s, eb):
                pe.wait_ge(hy_ready, s + 1)
                if later(s - 1):
                    pe.wait_ge(out_ready, s - 1)
                for t in range(TT):
                    last = pe.transpose(po[:, eb % 2, t], hy[:, eb % 2, t * P:(t + 1) * P], ident[:])
                last.then_inc(turned_back, 1)

            pe.wait_ge(consts_ready, 4)
            pe.wait_ge(small_loaded, 5 * 16)
            small = flat(py[:])
            pe.transpose(small[:, 0:2 * EB], gate_rows[:], ident[0:2 * EB, 0:2 * EB])
            pe.wait_ge(bias_row_ready, 1)
            pe.transpose(small[:, 2 * EB:3 * EB], bias_row[:], ident[0:EB, 0:EB]).then_inc(cols_turned, 1)
            turn_w(0)

            def group(g, r, q):
                slot = r % 2
                for eb in range(EB):
                    s = g * EB + eb
                    turns = 2 * q + r // 2 + 1 if eb == 0 else None
                    if later(s):
                        pe.wait_ge(z_ready, s)
                    if not later(g):
                        pe.wait_ge(w_lo_ready, 2 * eb + 2)
                    project(pz[:], 0, eb, slot, turns).then_inc(pz_done, 1)
                    if not later(g) and eb + 1 < EB:
                        turn_w(eb + 1)
                    if later(s - 1):
                        pe.wait_ge(b_ready, s - 1)
                    project(ph[:, eb % 2], 1, eb, slot, None).then_inc(ph_done, 1)
                    if later(s):
                        turn_back(s - 1, (eb - 1) % 4)
                        pe.wait_ge(y_ready, s)
                    else:
                        pe.wait_ge(cols_ready, 1)
                    if not later(g):
                        pe.wait_ge(kq_ready, eb + 1)
                    if eb == 0:
                        pe.wait_ge(q_turned[slot], turns * 16)
                    for kb in range(KB):
                        last = pe.matmul(py[:], kq[:, eb, kb], x_q[:, slot, :, kb], start=(kb == 0), stop=(kb == KB - 1))
                    last.then_inc(py_done, 1)

            all_groups(pe, group)
            turn_back(STEPS - 1, EB - 1)


_INS = ['L0_attn_x', 'L0_attn_Wz', 'L0_attn_bz', 'L0_attn_Wh', 'L0_attn_bh', 'L0_ffn_kernel',
        'L0_ffn_input_scale', 'L0_ffn_kernel_scale', 'L0_ffn_bias']


def kernel(**inputs):
    import numpy as _np
    import concourse.bacc as _bacc
    from concourse import mybir as _mybir
    from concourse.bass_utils import run_bass_kernel_spmd as _run

    nc = _bacc.Bacc("TRN2", target_bir_lowering=False, num_devices=1)
    arrays, args = {}, []
    for name in _INS:
        a = _np.ascontiguousarray(inputs[name])
        arrays[f"in_{name}_dram"] = a
        args.append(nc.dram_tensor(f"in_{name}_dram", a.shape, _mybir.dt.from_np(a.dtype), kind="ExternalInput").ap())
    shape = inputs['L0_attn_x'].shape
    args.append(nc.dram_tensor("out_dram", shape, _mybir.dt.float32, kind="ExternalOutput").ap())
    gated_scan_kernel(nc, *args)
    r = _run(nc, [arrays], core_ids=[0])
    return r.results[0]["out_dram"]
```

```python
from contextlib import ExitStack

import concourse.bass as bass
from concourse import mybir
from concourse.alu_op_type import AluOpType as ALU

ACT = mybir.ActivationFunctionType
AX_X = mybir.AxisListType.X
F32, F16, BF16 = mybir.dt.float32, mybir.dt.float16, mybir.dt.bfloat16
F8, U32, I32 = mybir.dt.float8e4, mybir.dt.uint32, mybir.dt.int32

P = 128
EPS = 1e-5
A_EPS = 1e-8
XN_SCALE = 2.0 ** 10
W_TOP = 2.0 ** 14
W_LEAST = 2.0 ** -40
EXPONENT = 0x7F800000
E4M3_LEAST = 2.0 ** -6
E4M3_ROUND = 1.5 * 2.0 ** 20
E4M3_OVER = 7.33e35
WARM_UP = 18
SAFE_S_IN_SQUARED = 2.0 ** -6


def later(value):
    return not isinstance(value, int) or value > 0


def gated_scan_kernel(nc, x_in, wz_in, bz_in, wh_in, bh_in, kern_in, s_in_in, s_k_in, bias_in, out):
    B, SEQ, D = x_in.shape
    E = wz_in.shape[0]
    GT = 512
    TT = GT // P
    KB = D // P
    EB = E // P
    G = B * SEQ // GT
    CHUNKS = SEQ // GT
    XR = B
    TILES, STEPS = TT * G, EB * G
    assert B == 4 and TT == 4 and KB == 4 and EB == 4 and G == 16 and CHUNKS == 4
    STATS_AHEAD, SPLIT_AHEAD = 7, 6
    FIRST_STATS = [[2], [3], [], [4], [5, 6], [7, 8], [9], [10]]
    FIRST_SPLIT = [[0, 1], [2], [3], [], [4], [5, 6], [7, 8], [9]]
    FIRST_LOW = [[0], [1], [2, 3], [], [4], [5, 6], [7, 8], [9]]

    with ExitStack() as ctx:
        def sb(name, shape, dt):
            return ctx.enter_context(nc.sbuf_tensor(name, shape, dt))

        def ps(name, shape, dt):
            return ctx.enter_context(nc.psum_tensor(name, shape, dt))

        def sem(name):
            return ctx.enter_context(nc.semaphore(name))

        x = sb("x_ring", [P, XR, TT, D], F32)
        wnat = sb("w_natural", [P, 2, EB, D], F32)
        kern = sb("kern", [P, KB, E], BF16)
        gate_rows = sb("gate_rows", [2 * EB, P], F32)
        bias_row16 = sb("bias_row16", [EB, P], BF16)
        bias_row = sb("bias_row", [EB, P], F32)
        scales = sb("scales", [P, 2], F32)
        ident = sb("ident", [P, P], F32)
        minus_half = sb("minus_half", [P, 1], F32)
        unused = sb("unused", [P, 1], F32)
        cols = sb("cols", [P, 3 * EB], F32)
        s_square = sb("s_square", [P, 1], F32)
        is_safe = sb("is_safe", [P, 1], I32)
        s_product = sb("s_product", [P, 1], F32)
        s_scaled = sb("s_scaled", [P, 2], F32)
        s_inverse = sb("s_inverse", [P, 2], F32)
        row_sum = sb("row_sum", [P, 2, EB], F32)
        row_pow = sb("row_pow", [P, 2, EB], F32)
        row_low = sb("row_low", [P, 2, EB], F32)
        row_inv = sb("row_inv", [P, 2, EB], F32)
        unscale = sb("unscale", [P, 2, EB], F32)
        bh_part = sb("bh_part", [P, EB], F32)
        bh_scaled = sb("bh_scaled", [P, EB], F32)
        w_hi = sb("w_hi", [P, 2, KB, E], F16)
        w_lo = sb("w_lo", [P, 2, KB, E], F16)
        kq = sb("kq", [P, EB, KB, P], BF16)
        kv = sb("kv", [P, EB, KB, P], F32)
        km = sb("km", [P, EB, KB, P], F32)
        qv = sb("qv", [P, D], F32)
        qm = sb("qm", [P, D], F32)
        qt = sb("qt", [P, D], F32)
        qr = sb("qr", [P, D], F32)
        stats = sb("stats", [P, 4, 6], F32)
        moments = sb("moments", [P, 4, 2], F32)
        var_eps = sb("var_eps", [P, 4], F32)
        rstd = sb("rstd", [P, 4], F32)
        mean_rstd = sb("mean_rstd", [P, 4], F32)
        shift = sb("shift", [P, 4], F32)
        xn = sb("xn", [P, 4, D], F32)
        n_hi = sb("n_hi", [P, 2, TT, D], F16)
        n_lo = sb("n_lo", [P, 2, TT, D], F16)
        n_q = sb("n_q", [P, 2, TT, D], BF16)
        n_bf = sb("n_bf", [P, 2, D], BF16)
        n_f8 = sb("n_f8", [P, 2, D], F8)
        x_hi = sb("x_hi", [P, 2, TT, KB, P], F16)
        x_lo = sb("x_lo", [P, 2, TT, KB, P], F16)
        x_q = sb("x_q", [P, 2, TT, KB, P], BF16)
        z = sb("z", [P, 2, GT], F32)
        one_minus_z = sb("one_minus_z", [P, 2, GT], F32)
        a = sb("a", [P, 2, GT], F32)
        b = sb("b", [P, 2, GT], F32)
        h = sb("h", [P, 2, GT], F32)
        h_last = sb("h_last", [P, B, EB], F32)
        y_bf = sb("y_bf", [P, 2, GT], BF16)
        y_biased = sb("y_biased", [P, 2, GT], BF16)
        hy = sb("hy", [P, 2, GT], F32)
        out_sb = sb("out_sb", [P, 2, TT, E], F32)

        pz = ps("pz", [P, TT, P], F32)
        ph = ps("ph", [P, 2, TT, P], F32)
        py = ps("py", [P, TT, P], F32)
        po = ps("po", [P, 2, TT, P], F32)
        pw = ps("pw", [P, 2, KB, P], F32)

        x_loaded = [sem(f"x_loaded{i}") for i in range(XR)]
        tile_loaded = [sem(f"tile{i}_loaded") for i in range(TT + 1)]
        w_loaded = [[sem(f"w{w}_loaded{i}") for i in range(EB)] for w in range(2)]
        kern_loaded = sem("kern_loaded")
        scales_loaded = sem("scales_loaded")
        rows_loaded = sem("rows_loaded")
        hi_turned = [sem(f"hi_turned{i}") for i in range(2)]
        lo_turned = [sem(f"lo_turned{i}") for i in range(2)]
        q_turned = [sem(f"q_turned{i}") for i in range(2)]
        first_hi_turned = sem("first_hi_turned")
        first_lo_turned = sem("first_lo_turned")
        stored = [sem(f"stored{i}") for i in range(2)]
        last_stored = [sem(f"last_stored{i}") for i in range(EB + 1)]
        consts_ready = sem("consts_ready")
        setup = sem("setup")
        scales_ready = sem("scales_ready")
        row_sums_ready = sem("row_sums_ready")
        w_scaled = sem("w_scaled")
        w_turned = sem("w_turned")
        w_hi_ready = sem("w_hi_ready")
        w_lo_ready = sem("w_lo_ready")
        bias_row_ready = sem("bias_row_ready")
        cols_turned = sem("cols_turned")
        cols_ready = sem("cols_ready")
        bh_ready = sem("bh_ready")
        kv_ready = sem("kv_ready")
        km_chain = sem("km_chain")
        km_ready = sem("km_ready")
        kq_chain = sem("kq_chain")
        kq_ready = sem("kq_ready")
        x_rounding = sem("x_rounding")
        sp_waited = sem("sp_waited")
        pool_waited = sem("pool_waited")
        dve_waited = sem("dve_waited")
        stats_done = sem("stats_done")
        moments_done = sem("moments_done")
        rstd_chain = sem("rstd_chain")
        shift_ready = sem("shift_ready")
        xn_ready = sem("xn_ready")
        n_bf_ready = sem("n_bf_ready")
        n_lo_ready = sem("n_lo_ready")
        n_bf_used = sem("n_bf_used")
        n_q_ready = sem("n_q_ready")
        pz_done = sem("pz_done")
        ph_done = sem("ph_done")
        py_done = sem("py_done")
        z_ready = sem("z_ready")
        one_minus_z_ready = sem("one_minus_z_ready")
        a_ready = sem("a_ready")
        b_ready = sem("b_ready")
        h_ready = sem("h_ready")
        h_last_ready = sem("h_last_ready")
        y_ready = sem("y_ready")
        y_biased_ready = sem("y_biased_ready")
        hy_ready = sem("hy_ready")
        turned_back = sem("turned_back")
        out_ready = sem("out_ready")
        ph_half_done = sem("ph_half_done")
        b_half_ready = sem("b_half_ready")
        h_half_ready = sem("h_half_ready")
        hy_half_ready = sem("hy_half_ready")
        half_turned_back = sem("half_turned_back")
        out_half_ready = sem("out_half_ready")

        def bits(ap):
            return ap.bitcast(U32)

        def flat(ap):
            return ap.rearrange("p t c -> p (t c)")

        HEAD = 2
        ROUNDS = (G - HEAD) // B

        def all_groups(eng, group):
            for g in range(HEAD):
                group(g, g % B, g // B)
            with eng.Fori(0, ROUNDS) as c:
                for j in range(HEAD, HEAD + B):
                    group(c * B + j, j % B, c + j // B)
            for g in range(HEAD + ROUNDS * B, G):
                group(g, g % B, g // B)

        def there(n, end):
            return not isinstance(n, int) or n < end

        def tiles_at(g, r, q, eb, ahead, first):
            s = g * EB + eb
            if isinstance(s, int) and s < len(first):
                return [(TT + t, t % TT, (TT + t) // TT % B, (TT + t) // TT // B) for t in first[s]]
            if not there(s + ahead, TILES):
                return []
            after = (eb + ahead) // TT
            return [(s + ahead, (eb + ahead) % TT, (r + after) % B, q + (r + after) // B)]

        HALVES = [slice(0, TT // 2), slice(TT // 2, TT)]

        def is_last(s):
            return isinstance(s, int) and s == STEPS - 1

        def x_rows(r, q):
            return x_in[r, bass.ds(q * GT, GT), :].rearrange("(t p) d -> p t d", p=P)

        def out_rows(r, q):
            return out[r, bass.ds(q * GT, GT), :].rearrange("(t p) d -> p t d", p=P)

        block = ctx.enter_context(nc.Block())

        @block.sync
        def _(sp):
            w_dram = [w.rearrange("(b p) d -> p b d", p=P) for w in (wz_in, wh_in)]

            def load_tile(t):
                sp.dma_start(x[:, t // TT, t % TT], x_in[t // TT, t % TT * P:(t % TT + 1) * P, :]).then_inc(
                    tile_loaded[t], 16)

            def load_w(eb):
                for w in range(2):
                    sp.dma_start(wnat[:, w, eb], w_dram[w][:, eb]).then_inc(w_loaded[w][eb], 16)

            load_tile(0)
            load_tile(1)
            load_w(0)
            load_tile(2)
            load_tile(3)
            sp.dma_start(kern[:], kern_in.rearrange("(k p) e -> p k e", p=P)).then_inc(kern_loaded, 16)
            load_w(1)
            sp.dma_start(gate_rows[0:EB], bz_in.rearrange("(b p) -> b p", p=P)).then_inc(rows_loaded, 16)
            sp.dma_start(gate_rows[EB:2 * EB], bh_in.rearrange("(b p) -> b p", p=P)).then_inc(rows_loaded, 16)
            sp.dma_start(bias_row16[:], bias_in.rearrange("(b p) -> b p", p=P)).then_inc(rows_loaded, 16)
            load_tile(TT)
            load_w(2)

            def turn_group(g, i):
                sp.wait_ge(n_bf_ready, g * TT + TT)
                sp.sem_inc(sp_waited, 1)
                if later(g * EB - EB):
                    sp.wait_ge(ph_done, g * EB - EB)
                sp.sem_inc(sp_waited, 1)
                sp.dma_start_transpose(x_hi[:, i].rearrange("p t k c -> p (t k) c"), flat(n_hi[:, i])).then_inc(hi_turned[i], 16)
                sp.wait_ge(n_lo_ready, g * TT + TT)
                sp.sem_inc(sp_waited, 1)
                sp.dma_start_transpose(x_lo[:, i].rearrange("p t k c -> p (t k) c"), flat(n_lo[:, i])).then_inc(lo_turned[i], 16)
                sp.wait_ge(n_q_ready, g * TT + TT)
                sp.sem_inc(sp_waited, 1)
                if later(g * EB - EB):
                    sp.wait_ge(py_done, g * EB - EB)
                sp.sem_inc(sp_waited, 1)
                sp.dma_start_transpose(x_q[:, i].rearrange("p t k c -> p (t k) c"), flat(n_q[:, i])).then_inc(q_turned[i], 16)

            def store(g, r, q):
                sp.wait_ge(out_ready, g * EB + EB)
                sp.sem_inc(sp_waited, 1)
                sp.dma_start(out_rows(r, q), out_sb[:, r % 2]).then_inc(stored[r % 2], 16)

            pair = TT // 2
            sp.wait_ge(n_bf_ready, pair)
            sp.dma_start_transpose(x_hi[:, 0, 0:pair].rearrange("p t k c -> p (t k) c"), flat(n_hi[:, 0, 0:pair])).then_inc(first_hi_turned, 16)
            sp.wait_ge(n_lo_ready, pair)
            sp.dma_start_transpose(x_lo[:, 0, 0:pair].rearrange("p t k c -> p (t k) c"), flat(n_lo[:, 0, 0:pair])).then_inc(first_lo_turned, 16)
            sp.wait_ge(n_bf_ready, TT)
            sp.dma_start_transpose(x_hi[:, 0, pair:TT].rearrange("p t k c -> p (t k) c"), flat(n_hi[:, 0, pair:TT])).then_inc(hi_turned[0], 16)
            sp.dma_start(x[:, 1, 1:TT], x_rows(1, 0)[:, 1:TT]).then_inc(x_loaded[1], 16)
            sp.wait_ge(n_lo_ready, TT)
            sp.dma_start_transpose(x_lo[:, 0, pair:TT].rearrange("p t k c -> p (t k) c"), flat(n_lo[:, 0, pair:TT])).then_inc(lo_turned[0], 16)
            sp.wait_ge(n_q_ready, TT)
            sp.dma_start_transpose(x_q[:, 0].rearrange("p t k c -> p (t k) c"), flat(n_q[:, 0])).then_inc(q_turned[0], 16)
            load_w(3)
            for r in range(2, XR):
                sp.dma_start(x[:, r], x_rows(r, 0)).then_inc(x_loaded[r], 16)
            turn_group(1, 1)

            def group(g, r, q):
                if later(g - 1) and there(g + 2, G):
                    sp.dma_start(x[:, (r + 2) % XR], x_rows((r + 2) % XR, q + (r + 2) // XR)).then_inc(
                        x_loaded[(r + 2) % XR], 16)
                if later(g):
                    if r:
                        store(g - 1, r - 1, q)
                    else:
                        store(g - 1, XR - 1, q - 1)
                    if there(g + 1, G):
                        turn_group(g + 1, (r + 1) % 2)

            all_groups(sp, group)
            last = G - 1
            rows = out_rows(last % B, last // B)
            for eb in range(EB - 1):
                cut = slice(eb * P, (eb + 1) * P)
                sp.wait_ge(out_ready, last * EB + eb + 1)
                sp.dma_start(rows[:, :, cut], out_sb[:, last % 2, :, cut]).then_inc(last_stored[eb], 16)
            cut = slice((EB - 1) * P, E)
            for half, tiles in enumerate(HALVES):
                sp.wait_ge(out_half_ready, half + 1)
                sp.dma_start(rows[:, tiles, cut], out_sb[:, last % 2, tiles, cut]).then_inc(
                    last_stored[EB - 1 + half], 16)
            sp.wait_ge(stored[0], 16 * (G // 2))
            sp.wait_ge(stored[1], 16 * (G // 2 - 1))
            for done in last_stored:
                sp.wait_ge(done, 16)

        @block.gpsimd
        def _(pool):
            nc.gpsimd.memset(ident[:], 0.0).then_inc(consts_ready, 1)
            nc.gpsimd.memset(minus_half[:], -0.5).then_inc(consts_ready, 1)
            nc.gpsimd.memset(h_last[:], 0.0).then_inc(consts_ready, 1)
            pool.wait_ge(consts_ready, 3)
            nc.gpsimd.affine_select(out=ident[:], in_=ident[:], compare_op=ALU.not_equal, fill=1.0, base=0,
                                    pattern=[[-1, P]], channel_multiplier=1).then_inc(consts_ready, 1)

            def scale_of_tile(t, i):
                pool.wait_ge(moments_done, t + 1)
                if later(t - 3):
                    pool.wait_ge(xn_ready, t - 3)
                pool.sem_inc(pool_waited, 1)
                nc.gpsimd.tensor_scalar(var_eps[:, i:i + 1], moments[:, i, 1:2], XN_SCALE ** -2, EPS * XN_SCALE ** -2,
                                        ALU.mult, ALU.add).then_inc(rstd_chain, 1)
                pool.wait_ge(rstd_chain, t * 3 + 1)
                nc.gpsimd.tensor_tensor(rstd[:, i:i + 1], var_eps[:, i:i + 1], minus_half[:], ALU.pow).then_inc(rstd_chain, 1)
                pool.wait_ge(rstd_chain, t * 3 + 2)
                nc.gpsimd.tensor_tensor(mean_rstd[:, i:i + 1], moments[:, i, 0:1], rstd[:, i:i + 1],
                                        ALU.mult).then_inc(rstd_chain, 1)
                pool.wait_ge(rstd_chain, t * 3 + 3)
                pool.sem_inc(pool_waited, 1)
                nc.gpsimd.tensor_scalar(shift[:, i:i + 1], mean_rstd[:, i:i + 1], -1.0, 0.0,
                                        ALU.mult, ALU.add).then_inc(shift_ready, 1)

            def round_kernel(eb):
                pool.wait_ge(km_ready, eb + 1)
                nc.gpsimd.tensor_tensor(kv[:, eb], kv[:, eb], km[:, eb], ALU.add).then_inc(kq_chain, 1)
                pool.wait_ge(kq_chain, eb * 3 + 1)
                nc.gpsimd.tensor_tensor(kv[:, eb], kv[:, eb], km[:, eb], ALU.subtract).then_inc(kq_chain, 1)
                pool.wait_ge(kq_chain, eb * 3 + 2)
                nc.gpsimd.tensor_scalar(km[:, eb], kv[:, eb], E4M3_OVER, 0.0, ALU.mult, ALU.mult).then_inc(kq_chain, 1)
                pool.wait_ge(kq_chain, eb * 3 + 3)
                nc.gpsimd.tensor_tensor(kq[:, eb], kv[:, eb], km[:, eb], ALU.add).then_inc(kq_ready, 1)

            for t in range(TT):
                scale_of_tile(t, t)
            scale_of_tile(TT, 0)
            round_kernel(0)
            scale_of_tile(TT + 1, 1)

            def group(g, r, q):
                for eb in range(EB):
                    s = g * EB + eb
                    pool.wait_ge(one_minus_z_ready, s + 1)
                    if later(s - 1):
                        pool.wait_ge(h_ready, s - 1)
                    pool.sem_inc(pool_waited, 1)
                    nc.gpsimd.tensor_scalar(a[:, eb % 2], one_minus_z[:, eb % 2], 1.0, A_EPS,
                                            ALU.mult, ALU.add).then_inc(a_ready, 1)
                    if not later(g) and eb + 1 < EB:
                        round_kernel(eb + 1)
                    for t, i, _, _ in tiles_at(g, r, q, eb, STATS_AHEAD, FIRST_STATS):
                        scale_of_tile(t, i)

            all_groups(pool, group)

        @block.scalar
        def _(act):
            act.dma_start(scales[:, 0:1], s_in_in.rearrange("(a b) -> a b", a=1).to_broadcast([P, 1])).then_inc(scales_loaded, 16)
            act.dma_start(scales[:, 1:2], s_k_in.rearrange("(a b) -> a b", a=1).to_broadcast([P, 1])).then_inc(scales_loaded, 16)
            act.wait_ge(consts_ready, 3)
            nc.scalar.activation(unused[:], minus_half[:], ACT.Sigmoid)

            def normalise(t, i, xslot):
                act.wait_ge(shift_ready, t + 1)
                if later(t - 3):
                    act.wait_ge(n_lo_ready, t - 3)
                nc.scalar.activation(xn[:, i], x[:, xslot, i], ACT.Identity, scale=rstd[:, i:i + 1],
                                     bias=shift[:, i:i + 1]).then_inc(xn_ready, 1)

            def high_parts(t, i, slot, turns):
                act.wait_ge(xn_ready, t + 1)
                if i == 0 and later(turns):
                    act.wait_ge(hi_turned[slot], turns * 16)
                    if slot == 0 and not later(turns - 1):
                        act.wait_ge(first_hi_turned, 16)
                nc.scalar.activation(n_hi[:, slot, i], xn[:, i], ACT.Copy)
                if later(t - 1):
                    act.wait_ge(n_bf_used, t - 1)
                nc.scalar.activation(n_bf[:, i % 2], xn[:, i], ACT.Copy).then_inc(n_bf_ready, 1)

            def sum_rows(eb):
                for w in range(2):
                    sum_row_block(w, eb)

            def sum_row_block(w, eb):
                act.wait_ge(w_loaded[w][eb], 16)
                aside = (x_q, x_lo)[w][:, 1, eb].rearrange("p k c -> p (k c)").bitcast(BF16)
                nc.scalar.activation(aside, wnat[:, w, eb], ACT.Abs,
                                     accum_out=row_sum[:, w, eb:eb + 1]).then_inc(row_sums_ready, 1)

            def split_w(eb):
                for w in range(2):
                    act.wait_ge(w_turned, 2 * eb + w + 1)
                    nc.scalar.activation(w_hi[:, w, :, eb * P:(eb + 1) * P], pw[:, w], ACT.Copy).then_inc(w_hi_ready, 1)

            def scale_kernel(eb):
                nc.scalar.activation(kv[:, eb], kern[:, :, eb * P:(eb + 1) * P], ACT.Copy,
                                     scale=s_inverse[:, 1:2]).then_inc(kv_ready, 1)

            sum_row_block(0, 0)
            normalise(0, 0, 0)
            sum_row_block(1, 0)
            high_parts(0, 0, 0, 0)
            for t in range(1, TT):
                normalise(t, t, 0)
                high_parts(t, t, 0, 0)
            act.wait_ge(scales_ready, 1)
            act.wait_ge(kern_loaded, 16)
            scale_kernel(0)
            split_w(0)
            sum_rows(1)
            scale_kernel(1)

            def group(g, r, q):
                for eb in range(EB):
                    s = g * EB + eb
                    tiles = tiles_at(g, r, q, eb, SPLIT_AHEAD, FIRST_SPLIT)
                    if not later(s):
                        (t, i, tr, tq), tiles = tiles[0], tiles[1:]
                        normalise(t, i, tr)
                        high_parts(t, i, tr % 2, 2 * tq + tr // 2)
                        sum_rows(2)
                    act.wait_ge(pz_done, s + 1)
                    if later(s - 1):
                        act.wait_ge(b_ready, s - 1)
                    else:
                        act.wait_ge(cols_ready, 1)
                    nc.scalar.activation(z[:, eb % 2], flat(pz[:]), ACT.Sigmoid, scale=unscale[:, 0, eb:eb + 1],
                                         bias=cols[:, eb:eb + 1]).then_inc(z_ready, 1)
                    if later(g):
                        for t, i, tr, tq in tiles:
                            normalise(t, i, tr)
                    act.wait_ge(z_ready, s + 1)
                    if later(s - 1):
                        act.wait_ge(a_ready, s - 1)
                    nc.scalar.activation(one_minus_z[:, eb % 2], z[:, eb % 2], ACT.Identity, scale=-1.0,
                                         bias=1.0).then_inc(one_minus_z_ready, 1)
                    if not later(g) and eb + 1 < EB:
                        split_w(eb + 1)
                    for t, i, tr, tq in tiles:
                        if not later(g):
                            normalise(t, i, tr)
                        high_parts(t, i, tr % 2, 2 * tq + tr // 2)
                    if not later(g) and eb + 2 < EB:
                        scale_kernel(eb + 2)
                    act.wait_ge(py_done, s + 1)
                    if later(s - 1):
                        act.wait_ge(y_biased_ready, s - 1)
                    nc.scalar.activation(y_bf[:, eb % 2], flat(py[:]), ACT.Copy, scale=s_product[:]).then_inc(y_ready, 1)
                    if not later(s):
                        sum_rows(3)

            all_groups(act, group)

        @block.vector
        def _(dve):
            v = nc.vector
            count = [0]

            def chain(ins):
                count[0] += 1
                ins.then_inc(setup, 1)
                dve.wait_ge(setup, count[0])

            def tile_stats(t, i, xslot):
                v.bn_stats(stats[:, i], x[:, xslot, i]).then_inc(stats_done, 1)

            def tile_moments(t, i):
                dve.wait_ge(stats_done, t + 1)
                if later(t - 3):
                    dve.wait_ge(shift_ready, t - 3)
                dve.sem_inc(dve_waited, 1)
                v.bn_aggr(moments[:, i], stats[:, i]).then_inc(moments_done, 1)

            def scale_w(eb):
                dve.wait_ge(row_sums_ready, 2 * eb + 2)
                chain(v.tensor_scalar(bits(row_pow[:, :, eb]), bits(row_sum[:, :, eb]), EXPONENT, None, ALU.bitwise_and))
                chain(v.tensor_scalar(row_low[:, :, eb], row_pow[:, :, eb], W_LEAST, None, ALU.max))
                chain(v.reciprocal(row_inv[:, :, eb], row_low[:, :, eb]))
                for w in range(2):
                    v.tensor_scalar(wnat[:, w, eb], wnat[:, w, eb], row_inv[:, w, eb:eb + 1], W_TOP,
                                    ALU.mult, ALU.mult).then_inc(w_scaled, 1)
                v.tensor_scalar(unscale[:, :, eb], row_low[:, :, eb], 1.0 / (W_TOP * XN_SCALE), None, ALU.mult)

            def split_w_lo(eb):
                for w in range(2):
                    cut = slice(eb * P, (eb + 1) * P)
                    dve.wait_ge(w_hi_ready, 2 * eb + w + 1)
                    v.tensor_tensor(w_lo[:, w, :, cut], pw[:, w], w_hi[:, w, :, cut], ALU.subtract).then_inc(w_lo_ready, 1)

            def scale_bh(eb):
                chain(v.tensor_tensor(bh_part[:, eb:eb + 1], cols[:, EB + eb:EB + eb + 1], row_inv[:, 1, eb:eb + 1],
                                      ALU.mult))
                v.tensor_scalar(bh_scaled[:, eb:eb + 1], bh_part[:, eb:eb + 1], W_TOP * XN_SCALE, None,
                                ALU.mult).then_inc(bh_ready, 1)

            def kernel_power(eb):
                dve.wait_ge(kv_ready, eb + 1)
                v.tensor_scalar(bits(km[:, eb]), bits(kv[:, eb]), EXPONENT, None, ALU.bitwise_and).then_inc(km_chain, 1)
                dve.wait_ge(km_chain, eb + 1)
                v.tensor_scalar(km[:, eb], km[:, eb], E4M3_LEAST, E4M3_ROUND, ALU.max, ALU.mult).then_inc(km_ready, 1)

            ROUNDING = 6

            def round_e4m3(dst, src, inverse, base):
                v.tensor_scalar(qv[:], src, inverse, None, ALU.mult).then_inc(x_rounding, 1)
                dve.wait_ge(x_rounding, base + 1)
                v.tensor_scalar(bits(qm[:]), bits(qv[:]), EXPONENT, None, ALU.bitwise_and).then_inc(x_rounding, 1)
                dve.wait_ge(x_rounding, base + 2)
                v.tensor_scalar(qt[:], qm[:], E4M3_LEAST, E4M3_ROUND, ALU.max, ALU.mult).then_inc(x_rounding, 1)
                dve.wait_ge(x_rounding, base + 3)
                v.tensor_tensor(qr[:], qv[:], qt[:], ALU.add).then_inc(x_rounding, 1)
                dve.wait_ge(x_rounding, base + 4)
                v.tensor_tensor(qm[:], qr[:], qt[:], ALU.subtract).then_inc(x_rounding, 1)
                dve.wait_ge(x_rounding, base + 5)
                v.tensor_scalar(qv[:], qm[:], E4M3_OVER, 0.0, ALU.mult, ALU.mult).then_inc(x_rounding, 1)
                dve.wait_ge(x_rounding, base + 6)
                return v.tensor_tensor(dst, qm[:], qv[:], ALU.add)

            def low_part(t, i, slot, turns):
                if i == 0 and later(turns):
                    dve.wait_ge(lo_turned[slot], turns * 16)
                    if slot == 0 and not later(turns - 1):
                        dve.wait_ge(first_lo_turned, 16)
                v.tensor_tensor(n_lo[:, slot, i], xn[:, i], n_hi[:, slot, i], ALU.subtract).then_inc(n_lo_ready, 1)

            def prepare(t, i, slot, turns):
                with dve.If(safe == 1):
                    dve.wait_ge(n_bf_ready, t + 1)
                    if later(t - 1):
                        dve.wait_ge(n_q_ready, t - 1)
                    dve.sem_inc(dve_waited, 1)
                    v.tensor_scalar(n_f8[:, i % 2], n_bf[:, i % 2], s_inverse[:, 0:1], None, ALU.mult,
                                    saturate=False).then_inc(n_bf_used, 1)
                    low_part(t, i, slot, turns)
                    dve.wait_ge(n_bf_used, t + 1)
                    if i == 0 and later(turns):
                        dve.wait_ge(q_turned[slot], turns * 16)
                    dve.sem_inc(dve_waited, 1)
                    v.tensor_copy(n_q[:, slot, i], n_f8[:, i % 2]).then_inc(n_q_ready, 1)
                with dve.Else():
                    dve.wait_ge(n_bf_ready, t + 1)
                    low_part(t, i, slot, turns)
                    if i == 0 and later(turns):
                        dve.wait_ge(q_turned[slot], turns * 16)
                    last = round_e4m3(n_q[:, slot, i], n_bf[:, i % 2], s_inverse[:, 0:1], t * ROUNDING)
                    last.then_inc(n_bf_used, 1)
                    dve.wait_ge(n_bf_used, t + 1)
                    dve.sem_inc(n_q_ready, 1)

            for t in range(2):
                dve.wait_ge(tile_loaded[t], 16)
                tile_stats(t, t, 0)
                tile_moments(t, t)

            dve.wait_ge(scales_loaded, 2 * 16)
            v.tensor_scalar(s_scaled[:, 0:1], scales[:, 0:1], XN_SCALE, None, ALU.mult)
            v.tensor_tensor(s_square[:], scales[:, 0:1], scales[:, 0:1], ALU.mult)
            chain(v.tensor_copy(s_scaled[:, 1:2], scales[:, 1:2]))
            v.reciprocal(s_inverse[:], s_scaled[:])
            v.tensor_tensor(s_product[:], scales[:, 0:1], scales[:, 1:2], ALU.mult).then_inc(scales_ready, 1)
            chain(v.tensor_scalar(is_safe[:], s_square[:], SAFE_S_IN_SQUARED, None, ALU.is_ge))
            safe = v.value_load(is_safe[0:1, 0:1], min_val=0, max_val=1)

            for t in range(2, TT):
                dve.wait_ge(tile_loaded[t], 16)
                tile_stats(t, t, 0)
                tile_moments(t, t)
            scale_w(0)
            prepare(0, 0, 0, 0)
            prepare(1, 1, 0, 0)
            dve.wait_ge(rows_loaded, 3 * 16)
            v.tensor_copy(bias_row[:], bias_row16[:]).then_inc(bias_row_ready, 1)
            prepare(2, 2, 0, 0)
            dve.wait_ge(tile_loaded[TT], 16)
            tile_stats(TT, 0, 1)
            tile_moments(TT, 0)
            prepare(3, 3, 0, 0)
            split_w_lo(0)
            kernel_power(0)
            dve.wait_ge(cols_turned, 1)
            v.tensor_copy(cols[:], flat(py[:])[:, 0:3 * EB]).then_inc(cols_ready, 1)
            dve.wait_ge(cols_ready, 1)
            scale_bh(0)
            scale_w(1)
            kernel_power(1)
            dve.wait_ge(x_loaded[1], 16)
            tile_stats(TT + 1, 1, 1)
            tile_moments(TT + 1, 1)

            def add_x(s, eb, r, q):
                dve.wait_ge(turned_back, s + 1)
                if eb == 0 and later(q * 2 + r // 2):
                    dve.wait_ge(stored[r % 2], (q * 2 + r // 2) * 16)
                cut = slice(eb * P, (eb + 1) * P)
                v.tensor_tensor(out_sb[:, r % 2, :, cut], x[:, r, :, cut], po[:, eb % 2], ALU.add).then_inc(out_ready, 1)

            def last_step(s, eb, r, q):
                add_x(s - 1, eb - 1, r, q)
                dve.wait_ge(y_ready, s + 1)
                v.tensor_scalar(y_biased[:, eb % 2], y_bf[:, eb % 2], cols[:, 2 * EB + eb:2 * EB + eb + 1], None,
                                ALU.add).then_inc(y_biased_ready, 1)
                dve.wait_ge(z_ready, s + 1)
                dve.wait_ge(a_ready, s + 1)
                dve.wait_ge(turned_back, s - 1)
                start = h_last[:, r, eb:eb + 1]
                for half, tiles in enumerate(HALVES):
                    tokens = slice(tiles.start * P, tiles.stop * P)
                    dve.wait_ge(ph_half_done, half + 1)
                    v.scalar_tensor_tensor(b[:, eb % 2, tokens], flat(ph[:, (eb + half) % 2, tiles]),
                                           bh_scaled[:, eb:eb + 1], z[:, eb % 2, tokens],
                                           ALU.add, ALU.mult).then_inc(b_half_ready, 1)
                    dve.wait_ge(b_half_ready, half + 1)
                    v.tensor_tensor_scan(h[:, eb % 2, tokens], a[:, eb % 2, tokens], b[:, eb % 2, tokens], start,
                                         ALU.mult, ALU.add).then_inc(h_half_ready, 1)
                    start = h[:, eb % 2, tokens.stop - 1:tokens.stop]
                    dve.wait_ge(h_half_ready, half + 1)
                    dve.wait_ge(y_biased_ready, s + 1)
                    v.scalar_tensor_tensor(hy[:, eb % 2, tokens], h[:, eb % 2, tokens], unscale[:, 1, eb:eb + 1],
                                           y_biased[:, eb % 2, tokens], ALU.mult, ALU.add).then_inc(hy_half_ready, 1)
                cut = slice(eb * P, (eb + 1) * P)
                for half, tiles in enumerate(HALVES):
                    dve.wait_ge(half_turned_back, half + 1)
                    v.tensor_tensor(out_sb[:, r % 2, tiles, cut], x[:, r, tiles, cut], po[:, (eb + half) % 2, tiles],
                                    ALU.add).then_inc(out_half_ready, 1)

            def group(g, r, q):
                for eb in range(EB):
                    s = g * EB + eb
                    to_measure = tiles_at(g, r, q, eb, STATS_AHEAD, FIRST_STATS)
                    to_split = tiles_at(g, r, q, eb, SPLIT_AHEAD, FIRST_LOW)
                    if not later(s):
                        for t, i, tr, tq in to_split:
                            prepare(t, i, tr % 2, 2 * tq + tr // 2)
                    if not later(g) and eb + 1 < EB:
                        split_w_lo(eb + 1)
                        scale_bh(eb + 1)
                        if eb == 1:
                            for t, i, tr, tq in to_measure:
                                tile_stats(t, i, tr)
                                tile_moments(t, i)
                            to_measure = []
                        if eb + 2 < EB:
                            scale_w(eb + 2)
                        if later(s):
                            (t, i, tr, tq), to_split = to_split[0], to_split[1:]
                            prepare(t, i, tr % 2, 2 * tq + tr // 2)
                    if is_last(s):
                        last_step(s, eb, r, q)
                        continue
                    dve.wait_ge(ph_done, s + 1)
                    dve.wait_ge(z_ready, s + 1)
                    if not later(g):
                        dve.wait_ge(bh_ready, eb + 1)
                    v.scalar_tensor_tensor(b[:, eb % 2], flat(ph[:, eb % 2]), bh_scaled[:, eb:eb + 1], z[:, eb % 2],
                                           ALU.add, ALU.mult).then_inc(b_ready, 1)
                    for t, i, tr, tq in to_measure[:1]:
                        if i == 0:
                            dve.wait_ge(x_loaded[tr], (tq + 1 - FIRST[tr]) * 16)
                        tile_stats(t, i, tr)
                    if later(s):
                        if eb:
                            add_x(s - 1, eb - 1, r, q)
                        elif r:
                            add_x(s - 1, EB - 1, r - 1, q)
                        else:
                            add_x(s - 1, EB - 1, B - 1, q - 1)
                    dve.wait_ge(a_ready, s + 1)
                    dve.wait_ge(b_ready, s + 1)
                    if later(s - 3):
                        dve.wait_ge(h_last_ready, s - 3)
                    v.tensor_tensor_scan(h[:, eb % 2], a[:, eb % 2], b[:, eb % 2], h_last[:, r, eb:eb + 1],
                                         ALU.mult, ALU.add).then_inc(h_ready, 1)
                    for t, i, tr, tq in to_measure[:1]:
                        tile_moments(t, i)
                    dve.wait_ge(y_ready, s + 1)
                    v.tensor_scalar(y_biased[:, eb % 2], y_bf[:, eb % 2], cols[:, 2 * EB + eb:2 * EB + eb + 1], None,
                                    ALU.add).then_inc(y_biased_ready, 1)
                    dve.wait_ge(h_ready, s + 1)
                    dve.wait_ge(y_biased_ready, s + 1)
                    if later(s - 1):
                        dve.wait_ge(turned_back, s - 1)
                    v.scalar_tensor_tensor(hy[:, eb % 2], h[:, eb % 2], unscale[:, 1, eb:eb + 1],
                                           y_biased[:, eb % 2], ALU.mult, ALU.add).then_inc(hy_ready, 1)
                    v.tensor_copy(h_last[:, r, eb:eb + 1], h[:, eb % 2, GT - 1:GT]).then_inc(h_last_ready, 1)
                    if not later(g) and eb + 2 < EB:
                        kernel_power(eb + 2)
                    for t, i, tr, tq in to_measure[1:]:
                        tile_stats(t, i, tr)
                        tile_moments(t, i)
                    if later(s):
                        for t, i, tr, tq in to_split:
                            prepare(t, i, tr % 2, 2 * tq + tr // 2)

            FIRST = [1] + [0] * (XR - 1)
            all_groups(dve, group)

        @block.tensor
        def _(pe):
            def turn_w(eb):
                for w in range(2):
                    pe.wait_ge(w_scaled, 2 * eb + w + 1)
                    if eb:
                        pe.wait_ge(w_lo_ready, 2 * eb + w - 1)
                    for kb in range(KB):
                        last = pe.transpose(pw[:, w, kb], wnat[:, w, eb, kb * P:(kb + 1) * P], ident[:])
                    last.then_inc(w_turned, 1)

            def project_hi(dst, w, eb, slot, tiles=slice(0, TT)):
                cut = slice(eb * P, (eb + 1) * P)
                for kb in range(KB):
                    pe.matmul(dst, w_hi[:, w, kb, cut], x_hi[:, slot, tiles, kb], start=(kb == 0), stop=False)
                    pe.matmul(dst, w_lo[:, w, kb, cut], x_hi[:, slot, tiles, kb], start=False, stop=False)

            def project_lo(dst, w, eb, slot, tiles=slice(0, TT)):
                cut = slice(eb * P, (eb + 1) * P)
                for kb in range(KB):
                    last = pe.matmul(dst, w_hi[:, w, kb, cut], x_lo[:, slot, tiles, kb], start=False, stop=(kb == KB - 1))
                return last

            def project_y(eb, slot):
                for kb in range(KB):
                    last = pe.matmul(py[:], kq[:, eb, kb], x_q[:, slot, :, kb], start=(kb == 0), stop=(kb == KB - 1))
                last.then_inc(py_done, 1)

            def last_step(s, eb, slot):
                turn_back(s - 1, eb - 1)
                pe.wait_ge(y_ready, s)
                project_y(eb, slot)
                for half, tiles in enumerate(HALVES):
                    if half:
                        pe.wait_ge(b_ready, s)
                    project_hi(ph[:, (eb + half) % 2, tiles], 1, eb, slot, tiles)
                    project_lo(ph[:, (eb + half) % 2, tiles], 1, eb, slot, tiles).then_inc(ph_half_done, 1)
                for half, tiles in enumerate(HALVES):
                    pe.wait_ge(hy_half_ready, half + 1)
                    pe.wait_ge(out_ready, s - 1 + half)
                    for t in range(tiles.start, tiles.stop):
                        last = pe.transpose(po[:, (eb + half) % 2, t], hy[:, eb % 2, t * P:(t + 1) * P], ident[:])
                    last.then_inc(half_turned_back, 1)

            def turn_back(s, eb):
                pe.wait_ge(hy_ready, s + 1)
                if later(s - 1):
                    pe.wait_ge(out_ready, s - 1)
                for t in range(TT):
                    last = pe.transpose(po[:, eb % 2, t], hy[:, eb % 2, t * P:(t + 1) * P], ident[:])
                last.then_inc(turned_back, 1)

            pe.wait_ge(consts_ready, 4)
            turn_w(0)
            pe.wait_ge(rows_loaded, 3 * 16)
            small = flat(py[:])
            pe.transpose(small[:, 0:2 * EB], gate_rows[:], ident[0:2 * EB, 0:2 * EB])
            pe.wait_ge(bias_row_ready, 1)
            pe.transpose(small[:, 2 * EB:3 * EB], bias_row[:], ident[0:EB, 0:EB]).then_inc(cols_turned, 1)
            for _ in range(WARM_UP):
                pe.transpose(pz[:, 0], ident[:], ident[:])

            def group(g, r, q):
                slot = r % 2
                turns = 2 * q + r // 2 + 1
                for eb in range(EB):
                    s = g * EB + eb
                    if later(s):
                        pe.wait_ge(z_ready, s)
                    if not later(g):
                        pe.wait_ge(w_lo_ready, 2 * eb + 1)
                    if eb == 0:
                        pe.wait_ge(hi_turned[slot], turns * 16)
                        if not later(g):
                            pe.wait_ge(first_hi_turned, 16)
                    project_hi(pz[:], 0, eb, slot)
                    if eb:
                        project_lo(pz[:], 0, eb, slot).then_inc(pz_done, 1)
                        if not later(g) and eb + 1 < EB:
                            turn_w(eb + 1)
                    if not later(g):
                        pe.wait_ge(w_lo_ready, 2 * eb + 2)
                    if later(s - 1):
                        pe.wait_ge(b_ready, s - 1)
                    if is_last(s):
                        last_step(s, eb, slot)
                        continue
                    project_hi(ph[:, eb % 2], 1, eb, slot)
                    if eb == 0:
                        pe.wait_ge(lo_turned[slot], turns * 16)
                        if not later(g):
                            pe.wait_ge(first_lo_turned, 16)
                        project_lo(pz[:], 0, eb, slot).then_inc(pz_done, 1)
                    project_lo(ph[:, eb % 2], 1, eb, slot).then_inc(ph_done, 1)
                    if later(s):
                        turn_back(s - 1, (eb - 1) % 4)
                        pe.wait_ge(y_ready, s)
                    else:
                        turn_w(1)
                        pe.wait_ge(cols_ready, 1)
                    if not later(g):
                        pe.wait_ge(kq_ready, eb + 1)
                    if eb == 0:
                        pe.wait_ge(q_turned[slot], turns * 16)
                    project_y(eb, slot)

            all_groups(pe, group)


_INS = ['L0_attn_x', 'L0_attn_Wz', 'L0_attn_bz', 'L0_attn_Wh', 'L0_attn_bh', 'L0_ffn_kernel',
        'L0_ffn_input_scale', 'L0_ffn_kernel_scale', 'L0_ffn_bias']


def kernel(**inputs):
    import numpy as _np
    import concourse.bacc as _bacc
    from concourse import mybir as _mybir
    from concourse.bass_utils import run_bass_kernel_spmd as _run

    nc = _bacc.Bacc("TRN2", target_bir_lowering=False, num_devices=1)
    arrays, args = {}, []
    for name in _INS:
        a = _np.ascontiguousarray(inputs[name])
        arrays[f"in_{name}_dram"] = a
        args.append(nc.dram_tensor(f"in_{name}_dram", a.shape, _mybir.dt.from_np(a.dtype), kind="ExternalInput").ap())
    shape = inputs['L0_attn_x'].shape
    args.append(nc.dram_tensor("out_dram", shape, _mybir.dt.float32, kind="ExternalOutput").ap())
    gated_scan_kernel(nc, *args)
    r = _run(nc, [arrays], core_ids=[0])
    return r.results[0]["out_dram"]
```
